# Optimizing a Trainium2 kernel written in Bass

```python
import numpy as np
import jax
import jax.numpy as jnp

def _softmax(x, axis=-1):
    return jax.nn.softmax(x, axis=axis)

def _gelu(x):
    return jax.nn.gelu(x, approximate=True)

def _silu(x):
    return jax.nn.silu(x)

def _sigmoid(x):
    return jax.nn.sigmoid(x)

def _layernorm(x, axis=-1, eps=1e-05):
    m = jnp.mean(x, axis=axis, keepdims=True)
    v = jnp.var(x, axis=axis, keepdims=True)
    return (x - m) / jnp.sqrt(v + eps)

def _scatter_add(tgt, idx, src, axis=0):
    return tgt.at[idx].add(src)

def _segment_sum(src, seg, n):
    return jax.ops.segment_sum(src, seg, n)
kernel_name = 'mk_decoder_postln_d1_seqx_r8_0bf160'

def setup_inputs(seed: int=0):
    np.random.seed(seed)
    _w = jnp.asarray

    def _rec_inputs():
        import jax
        import jax.numpy as jnp
        _rk = jax.random.key(seed)
        x = -0.0002928 + 1 * jax.random.normal(jax.random.fold_in(_rk, 1), (8, 128, 512), jnp.float32)
        _lenS = 128 - jax.random.randint(jax.random.fold_in(_rk, 7), (8,), 0, max(1, 128 // 4) + 1, jnp.int32)
        _lenS2 = 128 - jax.random.randint(jax.random.fold_in(_rk, 8), (8,), 0, max(1, 128 // 4) + 1, jnp.int32)
        _ctx_4096P = jax.random.normal(jax.random.fold_in(_rk, 11), (8, 16, 512), jnp.float32)
        _ctx_4096c = jax.random.dirichlet(jax.random.fold_in(_rk, 511), 0.3 * jnp.ones((16,), jnp.float32), (8, 128))
        _ctx_4096t = jnp.einsum('bsk,bkd->bsd', _ctx_4096c, _ctx_4096P)
        _ctx_4096t = _ctx_4096t * jax.lax.rsqrt(jnp.mean(jnp.square(_ctx_4096t)) + 1e-12) * 0.953939
        ctx_4096 = -2.8382e-05 + 0.999851 * (_ctx_4096t + 0.3 * jax.random.normal(jax.random.fold_in(_rk, 611), (8, 128, 512), jnp.float32))
        _validS = jnp.arange(128)[None, :] < _lenS[:, None]
        _validS2 = jnp.arange(128)[None, :] < _lenS2[:, None]
        _causal = jnp.tril(jnp.ones((128, 128), dtype=bool))
        mask_1x1xSxS2_ff0 = jnp.where(jnp.ones((1, 1, 128, 128), dtype=bool), 0.0, -1000000000.0).astype(jnp.float32)
        return (x, ctx_4096, mask_1x1xSxS2_ff0)
    x, ctx_4096, mask_1x1xSxS2_ff0 = _rec_inputs()

    def _L0_attn_setup():
        import jax, jax.numpy as jnp
        import numpy as np
        B, C, L = (64, 64, 512)
        key = jax.random.key(seed)
        x = jax.random.normal(key, (B, C, L), dtype=jnp.float32)
        return {'x': x}
    _L0_attn_all = _L0_attn_setup()
    _L0_attn_in = {k: v for k, v in _L0_attn_all.items() if k in ()}
    del _L0_attn_all

    def _L0_xattn_setup():
        import jax, jax.numpy as jnp
        import numpy as np
        NUM_HEADS = 32
        NUM_KV_HEADS = 8
        HEAD_DIM = 128
        HIDDEN = 512
        EPS = 1e-05

        def rmsnorm(x, w, eps=EPS):
            xf = x.astype(jnp.float32)
            var = jnp.mean(xf * xf, axis=-1, keepdims=True)
            return w * (xf * jax.lax.rsqrt(var + eps)).astype(x.dtype)
        key = jax.random.key(seed)
        ks = jax.random.split(key, 10)
        B, Q, KV = (1, 128, 6404)
        s = 1.0 / np.sqrt(HIDDEN)
        return {'hidden_states': jax.random.normal(ks[0], (B, Q, HIDDEN), jnp.float32), 'cross_attention_states': jax.random.normal(ks[1], (B, KV, HIDDEN), jnp.float32), 'attention_mask': jnp.zeros((B, 1, Q, KV), jnp.float32), 'q_proj_w': jax.random.normal(ks[2], (NUM_HEADS * HEAD_DIM, HIDDEN), jnp.float32) * s, 'k_proj_w': jax.random.normal(ks[3], (NUM_KV_HEADS * HEAD_DIM, HIDDEN), jnp.float32) * s, 'v_proj_w': jax.random.normal(ks[4], (NUM_KV_HEADS * HEAD_DIM, HIDDEN), jnp.float32) * s, 'o_proj_w': jax.random.normal(ks[5], (HIDDEN, NUM_HEADS * HEAD_DIM), jnp.float32) * s, 'q_norm_w': jnp.ones((HEAD_DIM,), jnp.float32), 'k_norm_w': jnp.ones((HEAD_DIM,), jnp.float32)}
    _L0_xattn_all = _L0_xattn_setup()
    _L0_xattn_in = {k: v for k, v in _L0_xattn_all.items() if k in ('q_proj_w', 'k_proj_w', 'v_proj_w', 'o_proj_w', 'q_norm_w', 'k_norm_w')}
    del _L0_xattn_all

    def _L0_ffn_setup():
        import jax, jax.numpy as jnp
        import numpy as np
        B, S, D = (4, 256, 512)
        NUM_EXPERTS, TOP_K = (3, 2)

        def _expert_outputs(h, w1, b1, w2, b2):
            pre = jnp.einsum('bsd,edf->ebsf', h, w1) + b1[:, None, None, :]
            act = jnp.stack([jnp.tanh(pre[0]), jax.nn.gelu(pre[1], approximate=False), jax.nn.silu(pre[2])])
            return jnp.einsum('ebsf,efd->ebsd', act, w2) + b2[:, None, None, :]
        key = jax.random.key(seed)
        ks = jax.random.split(key, 8)
        scale_in = 1.0 / np.sqrt(D)
        scale_gate = 1.0 / np.sqrt(D + 1)
        return {'h': jax.random.normal(ks[0], (B, S, D), dtype=jnp.float32), 'gate_w': jax.random.uniform(ks[1], (D + 1, NUM_EXPERTS), minval=-scale_gate, maxval=scale_gate, dtype=jnp.float32), 'gate_b': jnp.zeros((NUM_EXPERTS,), dtype=jnp.float32), 'w1': jax.random.uniform(ks[2], (NUM_EXPERTS, D, D), minval=-scale_in, maxval=scale_in, dtype=jnp.float32), 'b1': jnp.zeros((NUM_EXPERTS, D), dtype=jnp.float32), 'w2': jax.random.uniform(ks[3], (NUM_EXPERTS, D, D), minval=-scale_in, maxval=scale_in, dtype=jnp.float32), 'b2': jnp.zeros((NUM_EXPERTS, D), dtype=jnp.float32)}
    _L0_ffn_all = _L0_ffn_setup()
    _L0_ffn_in = {k: v for k, v in _L0_ffn_all.items() if k in ('gate_w', 'gate_b', 'w1', 'b1', 'w2', 'b2')}
    del _L0_ffn_all
    return {'x': x, 'ctx_4096': ctx_4096, 'mask_1x1xSxS2_ff0': mask_1x1xSxS2_ff0, 'L0_xattn_q_proj_w': _L0_xattn_in['q_proj_w'], 'L0_xattn_k_proj_w': _L0_xattn_in['k_proj_w'], 'L0_xattn_v_proj_w': _L0_xattn_in['v_proj_w'], 'L0_xattn_o_proj_w': _L0_xattn_in['o_proj_w'], 'L0_xattn_q_norm_w': _L0_xattn_in['q_norm_w'], 'L0_xattn_k_norm_w': _L0_xattn_in['k_norm_w'], 'L0_ffn_gate_w': _L0_ffn_in['gate_w'], 'L0_ffn_gate_b': _L0_ffn_in['gate_b'], 'L0_ffn_w1': _L0_ffn_in['w1'], 'L0_ffn_b1': _L0_ffn_in['b1'], 'L0_ffn_w2': _L0_ffn_in['w2'], 'L0_ffn_b2': _L0_ffn_in['b2']}

def reference(x, ctx_4096, mask_1x1xSxS2_ff0, L0_xattn_q_proj_w, L0_xattn_k_proj_w, L0_xattn_v_proj_w, L0_xattn_o_proj_w, L0_xattn_q_norm_w, L0_xattn_k_norm_w, L0_ffn_gate_w, L0_ffn_gate_b, L0_ffn_w1, L0_ffn_b1, L0_ffn_w2, L0_ffn_b2):
    import jax
    import jax.numpy as jnp

    def _L0_attn_ref(x):
        import jax, jax.numpy as jnp
        import numpy as np
        B, C, L = (64, 64, 512)
        b, c, l = x.shape
        q = jnp.transpose(x, (2, 0, 1))
        scale = jnp.asarray(c, x.dtype) ** 0.5
        scores = jnp.einsum('lnc,lmc->lnm', q, q) / scale
        prob = jax.nn.softmax(scores, axis=-1)
        msg = jnp.einsum('lnm,lmc->lnc', prob, q)
        return x + jnp.transpose(msg, (1, 2, 0))

    def _L0_xattn_ref(hidden_states, cross_attention_states, attention_mask, q_proj_w, k_proj_w, v_proj_w, o_proj_w, q_norm_w, k_norm_w):
        import jax, jax.numpy as jnp
        import numpy as np
        NUM_HEADS = 32
        NUM_KV_HEADS = 8
        HEAD_DIM = 128
        HIDDEN = 512
        EPS = 1e-05

        def rmsnorm(x, w, eps=EPS):
            xf = x.astype(jnp.float32)
            var = jnp.mean(xf * xf, axis=-1, keepdims=True)
            return w * (xf * jax.lax.rsqrt(var + eps)).astype(x.dtype)
        B, Q, _ = hidden_states.shape
        KV = cross_attention_states.shape[1]
        n_rep = NUM_HEADS // NUM_KV_HEADS
        q = (hidden_states @ q_proj_w.T).reshape(B, Q, NUM_HEADS, HEAD_DIM).transpose(0, 2, 1, 3)
        k = (cross_attention_states @ k_proj_w.T).reshape(B, KV, NUM_KV_HEADS, HEAD_DIM).transpose(0, 2, 1, 3)
        v = (cross_attention_states @ v_proj_w.T).reshape(B, KV, NUM_KV_HEADS, HEAD_DIM).transpose(0, 2, 1, 3)
        q = rmsnorm(q, q_norm_w)
        k = jnp.repeat(k, n_rep, axis=1)
        v = jnp.repeat(v, n_rep, axis=1)
        k = rmsnorm(k, k_norm_w)
        scale = 1.0 / np.sqrt(HEAD_DIM)
        scores = jnp.einsum('bhqd,bhkd->bhqk', q, k) * scale + attention_mask
        attn = jax.nn.softmax(scores.astype(jnp.float32), axis=-1).astype(q.dtype)
        out = jnp.einsum('bhqk,bhkd->bhqd', attn, v)
        out = out.transpose(0, 2, 1, 3).reshape(B, Q, NUM_HEADS * HEAD_DIM)
        return out @ o_proj_w.T

    def _L0_ffn_ref(h, gate_w, gate_b, w1, b1, w2, b2):
        import jax, jax.numpy as jnp
        import numpy as np
        B, S, D = (4, 256, 512)
        NUM_EXPERTS, TOP_K = (3, 2)

        def _expert_outputs(h, w1, b1, w2, b2):
            pre = jnp.einsum('bsd,edf->ebsf', h, w1) + b1[:, None, None, :]
            act = jnp.stack([jnp.tanh(pre[0]), jax.nn.gelu(pre[1], approximate=False), jax.nn.silu(pre[2])])
            return jnp.einsum('ebsf,efd->ebsd', act, w2) + b2[:, None, None, :]
        b, s, d = h.shape
        vision_len = int(s * 0.3)
        text_strength = jnp.mean(jnp.abs(h[:, vision_len:, :]), axis=(1, 2), keepdims=True)
        vision_strength = jnp.mean(jnp.abs(h[:, :vision_len, :]), axis=(1, 2), keepdims=True)
        modality_ratio = text_strength / (vision_strength + 1e-08)
        modality_ratio = jnp.broadcast_to(modality_ratio, (b, s, 1))
        router_input = jnp.concatenate([h, modality_ratio], axis=-1)
        gate_logits = router_input @ gate_w + gate_b
        gate_scores = jax.nn.softmax(gate_logits, axis=-1)
        top_val, top_idx = jax.lax.top_k(gate_scores, TOP_K)
        top_val = top_val / (jnp.sum(top_val, axis=-1, keepdims=True) + 1e-08)
        expert_out = _expert_outputs(h, w1, b1, w2, b2)
        moe_out = jnp.zeros_like(h)
        batch_idx = jnp.arange(b)
        for i in range(TOP_K):
            j = top_idx[:, 0, i]
            out_i = expert_out[j, batch_idx]
            moe_out = moe_out + top_val[..., i:i + 1] * out_i
        return moe_out
    x = _layernorm(x + _L0_attn_ref(x), axis=-1)
    x = _layernorm(x + _L0_xattn_ref(x, ctx_4096, mask_1x1xSxS2_ff0, L0_xattn_q_proj_w, L0_xattn_k_proj_w, L0_xattn_v_proj_w, L0_xattn_o_proj_w, L0_xattn_q_norm_w, L0_xattn_k_norm_w), axis=-1)
    x = _layernorm(x + _L0_ffn_ref(x, L0_ffn_gate_w, L0_ffn_gate_b, L0_ffn_w1, L0_ffn_b1, L0_ffn_w2, L0_ffn_b2), axis=-1)
    return x

_drawn_inputs = setup_inputs


def setup_inputs(seed=0):
    import zlib

    import numpy as np

    out = dict(_drawn_inputs(seed))
    spreads = {'L0_xattn_q_norm_w': (1.0, 0.2),
     'L0_xattn_k_norm_w': (1.0, 0.2),
     'L0_ffn_gate_b': (0.0, 0.1),
     'L0_ffn_b1': (0.0, 0.306),
     'L0_ffn_b2': (0.0, 0.1)}
    factors = {}
    for name, (base, spread) in spreads.items():
        noise = np.random.default_rng([zlib.crc32(name.encode()), seed]).standard_normal(out[name].shape)
        drawn = base * np.exp(spread * noise) if base else spread * noise
        out[name] = jnp.asarray(drawn.astype(out[name].dtype))
    for name, factor in factors.items():
        out[name] = (out[name] * factor).astype(out[name].dtype)
    return out
```

```python
from contextlib import ExitStack

import concourse.bass as bass
from concourse import mybir

F32 = mybir.dt.float32
F32R = mybir.dt.float32r
ACT = mybir.ActivationFunctionType
ALU = mybir.AluOpType
AX = mybir.AxisListType.X

P = 128
B = 8
D = 512
KT = D // P
T = B * P
HALF_T = T // 2
G = 8
R = 4
CH = 8
CG = 4
GL = 16
CL = CG * GL
E = 3
VIS = int(P * 0.3)
LEAD = 3
EPS = 1e-5
SELF_SCALE = float(P) ** -0.5
HEAD_SCALE = float(P) ** -0.5


class Chain:

    def __init__(self, eng, sem):
        self.eng, self.sem, self.base, self.n = eng, sem, 0, 0

    def __call__(self, ins):
        self.n += 1
        ins.then_inc(self.sem, 1)
        self.eng.wait_ge(self.sem, self.base + self.n)

    def turn(self, turns, per):
        self.ahead, self.per = self.n, per
        self.base, self.n = self.ahead + turns * per, 0

    def leave(self, turns):
        assert self.n == self.per, (self.n, self.per)
        self.base, self.n = 0, self.ahead + turns * self.per


class Semaphores:

    def __init__(self, sem):
        self.consts = sem("consts")
        self.const_dma = sem("const_dma")
        self.kv_hi_done = sem("kv_hi_done")
        self.kv_lo_done = sem("kv_lo_done")
        self.x_dma = sem("x_dma")
        self.ctx_hi_done = sem("ctx_hi_done")
        self.ctx_lo_done = sem("ctx_lo_done")
        self.a_scores = sem("a_scores")
        self.a_extracted = sem("a_extracted")
        self.a_sub = sem("a_sub")
        self.a_exp = sem("a_exp")
        self.a_probs = sem("a_probs")
        self.a_turned = sem("a_turned")
        self.a_probs_t = sem("a_probs_t")
        self.a_msg = sem("a_msg")
        self.a_added = sem("a_added")
        self.k_done = sem("k_done")
        self.k_saved_raw = sem("k_saved_raw")
        self.k_mean = sem("k_mean")
        self.k_rsqrt = sem("k_rsqrt")
        self.k_normed = sem("k_normed")
        self.k_turned = sem("k_turned")
        self.k_saved = sem("k_saved")
        self.v_done = sem("v_done")
        self.v_saved = sem("v_saved")
        self.ln_var = sem("ln_var")
        self.ln_rstd = sem("ln_rstd")
        self.ln_out = sem("ln_out")
        self.x_turned = sem("x_turned")
        self.x_hi_done = sem("x_hi_done")
        self.x_lo_done = sem("x_lo_done")
        self.wq_hi_done = sem("wq_hi_done")
        self.wq_lo_done = sem("wq_lo_done")
        self.wo_dma = sem("wo_dma")
        self.wo_hi_done = sem("wo_hi_done")
        self.wo_lo_done = sem("wo_lo_done")
        self.q_done = sem("q_done")
        self.q_saved = sem("q_saved")
        self.q_squared = sem("q_squared")
        self.q_summed = sem("q_summed")
        self.q_mean = sem("q_mean")
        self.q_rsqrt = sem("q_rsqrt")
        self.s_done = sem("s_done")
        self.s_masked = sem("s_masked")
        self.s_max = sem("s_max")
        self.s_exp = sem("s_exp")
        self.s_rsum = sem("s_rsum")
        self.p_done = sem("p_done")
        self.p_turned = sem("p_turned")
        self.p_saved = sem("p_saved")
        self.v_ready = sem("v_ready")
        self.pv_done = sem("pv_done")
        self.at_hi_done = sem("at_hi_done")
        self.at_lo_done = sem("at_lo_done")
        self.o_done = sem("o_done")
        self.o_added = sem("o_added")
        self.ff_hi_done = sem("ff_hi_done")
        self.ff_lo_done = sem("ff_lo_done")
        self.row_sums = sem("row_sums")
        self.means = sem("means")
        self.picked = sem("picked")
        self.choice_out = sem("choice_out")
        self.pre_done = sem("pre_done")
        self.act_done = sem("act_done")
        self.hid_hi_done = sem("hid_hi_done")
        self.hid_lo_done = sem("hid_lo_done")
        self.y_done = sem("y_done")
        self.y_added = sem("y_added")
        self.g_sub = sem("g_sub")
        self.g_exp = sem("g_exp")
        self.gate_in = sem("gate_in")
        self.store = sem("store")
        self.dve_link = sem("dve_link")
        self.pool_link = sem("pool_link")
        self.kv_dma = [sem(f"kv_dma{i}") for i in range(4)]
        self.ff_dma = [sem(f"ff_dma{i}") for i in range(4)]
        self.wq_dma = [sem(f"wq_dma{i}") for i in range(2)]
        self.cols_dma = [sem(f"cols_dma{i}") for i in range(2)]
        self.rows_dma = [sem(f"rows_dma{i}") for i in range(2)]
        self.ctx_dma = [sem(f"ctx_dma{i}") for i in range(2)]


def after(eng, sem, value):
    if not isinstance(value, int) or value > 0:
        eng.wait_ge(sem, value)


def build(nc, x_nat, x_cols, x_rows, ctx_t, mask, wq_t, wkv_t, wo_t, qn_w, kn_w,
          gate_wt, gate_last, gate_b, w1, b1_t, w2, b2, out):
    with ExitStack() as stack:
        base = (nc.sbuf_base + 63) // 64 * 64
        cur = [base]

        def sb(name, shape, dt=F32):
            size = 4
            for n in shape[1:]:
                size *= n
            t = nc.alloc_sbuf_tensor_at(name, shape, dt, offset=cur[0])
            cur[0] += (size + 31) // 32 * 32
            return t

        def bank(name):
            return stack.enter_context(nc.psum_tensor(name, [P, 512], F32))

        def sem(name):
            return stack.enter_context(nc.semaphore(name))

        ident = sb("ident", [P, P])
        blockmask = sb("blockmask", [P, P])
        mask_sb = sb("mask_sb", [P, P])
        text_mean = sb("text_mean", [P, P])
        vis_mean = sb("vis_mean", [P, P])
        row0 = sb("row0", [P, P])
        ones = sb("ones", [P, 1])
        neghalf = sb("neghalf", [P, 16])
        qn_b = sb("qn_b", [P, P])
        kn_b = sb("kn_b", [P, P])
        wqk = sb("wqk", [P, P])
        bn = sb("bn", [P, B, 6])
        mv = sb("mv", [P, B, 2])
        ve = sb("ve", [P, B])
        rstd = sb("rstd", [P, B])
        b1_sb = sb("b1_sb", [P, E, KT])
        gw_last = sb("gw_last", [P, E])
        gb_sb = sb("gb_sb", [P, E])
        q_ms = sb("q_ms", [P, R])
        q_rstd = sb("q_rstd", [P, 2, R, 4])
        neg_max = sb("neg_max", [P, R])
        esum = sb("esum", [P, R])
        rsum = sb("rsum", [P, R])
        x1 = sb("x1", [P, B, D])
        wq_raw = sb("wq_raw", [P, 2, KT * P])
        wo_raw = sb("wo_raw", [P, R, D])
        at_kv = cur[0]
        k_t = sb("k_t", [P, G, T])
        v_all = sb("v_all", [P, B, G * P])
        at_ac = cur[0]
        wkv_hi = sb("wkv_hi", [P, 2, KT, G * P], F32R)
        wkv_lo = sb("wkv_lo", [P, 2, KT, G * P], F32R)
        kv_raw = sb("kv_raw", [P, 4, 512])
        cols = sb("cols", [P, 2, 512])
        rows = sb("rows", [P, 2, 512])
        ctx_raw = sb("ctx_raw", [P, 2, 512])
        ctx_hi = sb("ctx_hi", [P, 512], F32R)
        ctx_lo = sb("ctx_lo", [P, 512], F32R)
        masked = sb("masked", [P, CG, P])
        block_p = sb("block_p", [P, CG, P])
        block_pt = sb("block_pt", [P, CG, P])
        sc = sb("sc", [P, CG, B])
        sc_max = sb("sc_max", [P, CG])
        sc_sub = sb("sc_sub", [P, CG, B])
        sc_exp = sb("sc_exp", [P, CG, B])
        sc_sum = sb("sc_sum", [P, CG])
        sc_rec = sb("sc_rec", [P, CG])
        sc_p = sb("sc_p", [P, CG, B])
        k_raw = sb("k_raw", [P, G, P])
        k_n = sb("k_n", [P, G, P])
        k_ss = sb("k_ss", [P, G])
        k_ms = sb("k_ms", [P, G])
        k_rstd = sb("k_rstd", [P, G])
        assert cur[0] <= nc.sbuf_usable_end, cur[0]
        cur[0] = at_ac
        x_hi = sb("x_hi", [P, KT, T], F32R)
        x_lo = sb("x_lo", [P, KT, T], F32R)
        q_t = sb("q_t", [P, 2, R, HALF_T])
        q_sq = sb("q_sq", [P, HALF_T])
        wq_hi = sb("wq_hi", [P, R, KT, P], F32R)
        wq_lo = sb("wq_lo", [P, R, KT, P], F32R)
        wo_hi = sb("wo_hi", [P, R, D], F32R)
        wo_lo = sb("wo_lo", [P, R, D], F32R)
        v_g = sb("v_g", [P, B, P])
        sx = sb("sx", [P, 2, R, P])
        pr = sb("pr", [P, 2, R, P])
        pr_t = sb("pr_t", [P, R, P])
        at_hi = sb("at_hi", [P, R, P], F32R)
        at_lo = sb("at_lo", [P, R, P], F32R)
        assert cur[0] <= nc.sbuf_usable_end, cur[0]
        cur[0] = at_kv
        w1_hi = [sb(f"w1_hi{e}", [P, KT, D], F32R) for e in range(E)]
        w1_lo = [sb(f"w1_lo{e}", [P, KT, D], F32R) for e in range(E)]
        x2_hi = sb("x2_hi", [P, KT, T], F32R)
        x2_lo = sb("x2_lo", [P, KT, T], F32R)
        w2_hi = [sb(f"w2_hi{e}", [P, KT, D], F32R) for e in range(E)]
        w2_lo = [sb(f"w2_lo{e}", [P, KT, D], F32R) for e in range(E)]
        ff_raw = wo_raw
        hid = sb("hid", [P, 2, HALF_T])
        hid_hi = sb("hid_hi", [P, KT, HALF_T], F32R)
        hid_lo = sb("hid_lo", [P, KT, HALF_T], F32R)
        b2_b = sb("b2_b", [P, E, D])
        gw_b = sb("gw_b", [P, E, D])
        junk = sb("junk", [P, D])
        row_abs = sb("row_abs", [P, B])
        gt = sb("gt", [P, 40, B])
        onehot = sb("onehot", [P, 2, E, B])
        choice = sb("choice", [P, 2, E, B])
        coef = sb("coef", [P, E, B])
        assert cur[0] <= nc.sbuf_usable_end, cur[0]

        pb = [bank(f"bank{i}") for i in range(8)]

        s = Semaphores(sem)
        kv_dma, ff_dma, wq_dma, cols_dma, rows_dma, ctx_dma = (
            s.kv_dma, s.ff_dma, s.wq_dma, s.cols_dma, s.rows_dma, s.ctx_dma)
        N_CONST_DMA = 6

        block = stack.enter_context(nc.Block())

        FF = [(w, e, k) for e in range(E) for w in (0, 1) for k in range(KT)]
        ff_index = {wek: n for n, wek in enumerate(FF)}

        @block.sync
        def _(sp):
            for n in range(4):
                sp.dma_start(kv_raw[:, n, :], wkv_t[n]).then_inc(kv_dma[n], 16)
            for u in range(2):
                sp.dma_start(cols[:, u, :], x_cols[u]).then_inc(cols_dma[u], 16)
                sp.dma_start(ctx_raw[:, u, :], ctx_t[u]).then_inc(ctx_dma[u], 16)
                sp.dma_start(rows[:, u, :], x_rows[u]).then_inc(rows_dma[u], 16)
            sp.dma_start(x1[:], x_nat.rearrange("b c l -> c b l")).then_inc(s.x_dma, 16)
            one = lambda a: a.rearrange("(a d) -> a d", a=1)
            for dst, src in (
                (mask_sb[:], mask), (qn_b[:], one(qn_w).to_broadcast([P, P])),
                (kn_b[:], one(kn_w).to_broadcast([P, P])), (b1_sb[:], b1_t),
                (gw_last[:], one(gate_last).to_broadcast([P, E])),
                (gb_sb[:], one(gate_b).to_broadcast([P, E])),
            ):
                sp.dma_start(dst, src).then_inc(s.const_dma, 16)
            for n in range(4, 16):
                sp.wait_ge(s.kv_lo_done, n - 3)
                sp.dma_start(kv_raw[:, n % 4, :], wkv_t[n]).then_inc(kv_dma[n % 4], 16)
            for m in range(2):
                sp.dma_start(wq_raw[:, m, :], wq_t[m]).then_inc(wq_dma[m], 16)
            sp.dma_start(wo_raw[:], wo_t[0]).then_inc(s.wo_dma, 16)
            with sp.Fori(0, CH // 2 - 1) as turn:
                for u in range(2):
                    i = 2 * turn + 2 + u
                    sp.wait_ge(s.a_scores, i - 1)
                    sp.dma_start(cols[:, u, :], x_cols[bass.ds(i, 1)].rearrange("a p n -> p (a n)")).then_inc(cols_dma[u], 16)
                    sp.wait_ge(s.ctx_lo_done, i - 1)
                    sp.dma_start(ctx_raw[:, u, :], ctx_t[bass.ds(i, 1)].rearrange("a p n -> p (a n)")).then_inc(ctx_dma[u], 16)
                    sp.wait_ge(s.a_msg, i - 1)
                    sp.dma_start(rows[:, u, :], x_rows[bass.ds(i, 1)].rearrange("a p n -> p (a n)")).then_inc(rows_dma[u], 16)
            for m in range(2, 4):
                sp.wait_ge(s.wq_lo_done, m - 1)
                sp.dma_start(wq_raw[:, m % 2, :], wq_t[m]).then_inc(wq_dma[m % 2], 16)
            with sp.Fori(0, G - 1) as g:
                for h in range(R):
                    m = 4 * g + 4 + h
                    sp.wait_ge(s.wq_lo_done, m - 1)
                    sp.dma_start(wq_raw[:, h % 2, :], wq_t[bass.ds(m, 1)].rearrange("a p n -> p (a n)")).then_inc(wq_dma[h % 2], 16)
                    if h == 1:
                        sp.wait_ge(s.wo_lo_done, 4 * g + 4)
                        sp.dma_start(wo_raw[:], wo_t[bass.ds(g + 1, 1)].rearrange("a p h n -> p (a h) n")).then_inc(s.wo_dma, 16)
            sp.wait_ge(s.o_added, G * B)
            for dst, src in ((gw_b[:], gate_wt), (b2_b[:], b2)):
                for e in range(E):
                    sp.dma_start(dst[:, e, :], src[e:e + 1, :].to_broadcast([P, D])).then_inc(s.gate_in, 16)
            for n, (w, e, k) in enumerate(FF):
                if n >= 4:
                    sp.wait_ge(s.ff_lo_done, n - 3)
                sp.dma_start(ff_raw[:, n % 4, :], (w1, w2)[w][e, k * P:(k + 1) * P, :]).then_inc(ff_dma[n % 4], 16)
            for b in range(B):
                sp.wait_ge(s.ln_out, 2 * B + b + 1)
                sp.dma_start(out[b], x1[:, b, :]).then_inc(s.store, 16)
            sp.wait_ge(s.store, 16 * B)

        @block.gpsimd
        def _(pool):
            link = Chain(pool, s.pool_link)
            link(pool.memset(ident[:], 1.0))
            link(pool.affine_select(out=ident[:], in_=ident[:], compare_op=ALU.is_equal, fill=0.0, base=0,
                                    pattern=[[-1, P]], channel_multiplier=1))
            bm = blockmask[:].rearrange("p (l m) -> p l m", m=B)
            link(pool.memset(blockmask[:], 1.0))
            link(pool.affine_select(out=bm, in_=bm, compare_op=ALU.is_ge, fill=0.0, base=0,
                                    pattern=[[-B, GL], [0, B]], channel_multiplier=1))
            link(pool.affine_select(out=bm, in_=bm, compare_op=ALU.is_ge, fill=0.0, base=B - 1,
                                    pattern=[[B, GL], [0, B]], channel_multiplier=-1))
            link(pool.memset(text_mean[:], 1.0 / ((P - VIS) * D)))
            link(pool.affine_select(out=text_mean[:], in_=text_mean[:], compare_op=ALU.is_ge, fill=0.0, base=-VIS,
                                    pattern=[[0, P]], channel_multiplier=1))
            link(pool.memset(vis_mean[:], 1.0 / (VIS * D)))
            link(pool.affine_select(out=vis_mean[:], in_=vis_mean[:], compare_op=ALU.is_ge, fill=0.0, base=VIS - 1,
                                    pattern=[[0, P]], channel_multiplier=-1))
            link(pool.memset(row0[:], 1.0))
            link(pool.affine_select(out=row0[:], in_=row0[:], compare_op=ALU.is_ge, fill=0.0, base=0,
                                    pattern=[[0, P]], channel_multiplier=-1))
            link(pool.memset(ones[:], 1.0))
            pool.memset(neghalf[:], -0.5).then_inc(s.consts, 1)
            pool.wait_ge(s.consts, 1)

            def rsqrt(dst, src, n):
                return pool.tensor_tensor(dst, src, neghalf[:, 0:n], ALU.pow)

            with pool.Fori(0, B) as i:
                pool.wait_ge(s.k_mean, i + 1)
                rsqrt(k_rstd[:], k_ms[:], G).then_inc(s.k_rsqrt, 1)

            def layer_norm_rsqrt(n):
                pool.wait_ge(s.ln_var, n + 1)
                rsqrt(rstd[:], ve[:], B).then_inc(s.ln_rstd, 1)

            layer_norm_rsqrt(0)

            def split_wq(g, h):
                pool.wait_ge(wq_dma[h % 2], 32 * g + 16 * (h // 2 + 1))
                raw = wq_raw[:, h % 2, :].rearrange("p (k d) -> p k d", k=KT)
                pool.tensor_tensor(wq_hi[:, h], raw, ones[:].unsqueeze(1).to_broadcast([P, KT, P]),
                                   ALU.mult).then_inc(s.wq_hi_done, 1)
                pool.wait_ge(s.wq_hi_done, 4 * g + h + 1)
                pool.tensor_tensor(wq_lo[:, h], raw, wq_hi[:, h], ALU.subtract).then_inc(s.wq_lo_done, 1)

            def copy_v(g, half):
                src = v_all[:, 4 * half:4 * half + 4, bass.ds(g * P, P)]
                pool.tensor_copy(v_g[:, 4 * half:4 * half + 4, :], src).then_inc(s.v_ready, 1)

            pool.wait_ge(s.x_lo_done, 1)
            for h in range(R):
                split_wq(0, h)
            copy_v(0, 0)

            def q_rsqrt(n, half, h):
                pool.wait_ge(s.q_mean, n + 1)
                rsqrt(q_rstd[:, half, h, :], q_ms[:, :], 4).then_inc(s.q_rsqrt, 1)

            for h in range(R):
                q_rsqrt(h, 0, h)

            def step(g, j, last=False):
                n = 8 * g + j + 4
                if 3 <= j < 7 and not last:
                    pool.wait_ge(s.q_done, 8 * g + j + 2)
                    split_wq(g + 1, j - 3)
                if j < 4:
                    q_rsqrt(n, 1, j)
                elif not last:
                    q_rsqrt(n, 0, j - 4)
                if j == 1:
                    after(pool, s.pv_done, 8 * g)
                    copy_v(g, 1)
                if j == 5 and not last:
                    pool.wait_ge(s.pv_done, 8 * g + 4)
                    copy_v(g + 1, 0)

            for j in range(LEAD):
                step(0, j)
            with pool.Fori(0, G - 1) as g:
                for j in range(LEAD, 8):
                    step(g, j)
                for j in range(LEAD):
                    step(g + 1, j)
            for j in range(LEAD, 8):
                step(G - 1, j, last=True)

            layer_norm_rsqrt(1)
            for n, (w, e, k) in enumerate(FF):
                pool.wait_ge(s.ff_hi_done, n + 1)
                hi, lo = ((w1_hi, w1_lo), (w2_hi, w2_lo))[w]
                pool.tensor_tensor(lo[e][:, k, :], ff_raw[:, n % 4, :], hi[e][:, k, :], ALU.subtract).then_inc(s.ff_lo_done, 1)
            layer_norm_rsqrt(2)

        @block.scalar
        def _(act):
            for n in range(16):
                act.wait_ge(kv_dma[n % 4], 16 * (n // 4 + 1))
                w, k, half = n // 8, n // 2 % 4, n % 2
                act.activation(wkv_hi[:, w, k, bass.ts(half, 512)], kv_raw[:, n % 4, :], ACT.Copy).then_inc(s.kv_hi_done, 1)

            def chunk(turn, u):
                i = 2 * turn + u
                act.wait_ge(ctx_dma[u], 16 * turn + 16)
                after(act, s.v_done, 2 * i)
                act.activation(ctx_hi[:], ctx_raw[:, u, :], ACT.Copy).then_inc(s.ctx_hi_done, 1)
                act.wait_ge(s.a_sub, i + 1)
                act.activation(sc_exp[:], sc_sub[:], ACT.Exp, scale=SELF_SCALE).then_inc(s.a_exp, 1)
                act.wait_ge(s.k_done, i + 1)
                after(act, s.k_normed, i)
                after(act, s.k_turned, 2 * i)
                for half in range(2):
                    for c in range(4):
                        act.activation(k_n[:, 4 * half + c, :], pb[3 + half][:, bass.ts(c, P)], ACT.Square,
                                       accum_out=k_ss[:, 4 * half + c:4 * half + c + 1])
                    ins = act.activation(k_raw[:, 4 * half:4 * half + 4, :], pb[3 + half][:], ACT.Copy)
                ins.then_inc(s.k_saved_raw, 1)
                act.wait_ge(s.v_done, 2 * i + 1)
                act.activation(v_all[:, bass.ds(i, 1), 0:512].rearrange("p a n -> p (a n)"), pb[5][:], ACT.Copy).then_inc(s.v_saved, 1)
                act.wait_ge(s.a_turned, i + 1)
                after(act, s.a_msg, i)
                act.activation(block_pt[:], pb[1][:], ACT.Copy).then_inc(s.a_probs_t, 1)
                act.wait_ge(s.v_done, 2 * i + 2)
                act.activation(v_all[:, bass.ds(i, 1), 512:1024].rearrange("p a n -> p (a n)"), pb[6][:], ACT.Copy).then_inc(s.v_saved, 1)
                for half in range(2):
                    act.wait_ge(s.k_turned, 2 * i + half + 1)
                    act.activation(k_t[:, 4 * half:4 * half + 4, bass.ds(i * P, P)], pb[(7, 1)[half]][:], ACT.Copy).then_inc(s.k_saved, 1)

            chunk(0, 0)
            chunk(0, 1)
            with act.Fori(1, CH // 2) as turn:
                chunk(turn, 0)
                chunk(turn, 1)

            def save_hi(n, hi):
                for b in range(B):
                    act.wait_ge(s.x_turned, B * n + b + 1)
                    act.activation(hi[:, :, bass.ts(b, P)], pb[b % 2][:].rearrange("p (k t) -> p k t", k=KT),
                                   ACT.Copy).then_inc(s.x_hi_done, 1)

            save_hi(0, x_hi)

            def save_q(n, half, h):
                act.wait_ge(s.q_done, n + 1)
                act.activation(q_t[:, half, h, :], pb[2][:], ACT.Copy).then_inc(s.q_saved, 1)

            def square_q(n):
                after(act, s.q_summed, n)
                act.activation(q_sq[:], pb[2][:], ACT.Square).then_inc(s.q_squared, 1)

            for h in range(R):
                save_q(h, 0, h)
                square_q(h)

            def exps(g, j):
                t = 8 * g + j
                act.wait_ge(s.s_max, t + 1)
                for h in range(R):
                    ins = act.activation(sx[:, j % 2, h, :], sx[:, j % 2, h, :], ACT.Exp, bias=neg_max[:, h:h + 1],
                                         accum_out=esum[:, h:h + 1])
                ins.then_inc(s.s_exp, 1)

            def save_p(t):
                act.wait_ge(s.p_turned, t + 1)
                after(act, s.pv_done, t)
                act.activation(pr_t[:], pb[1][:], ACT.Copy).then_inc(s.p_saved, 1)

            def save_attention(t):
                act.wait_ge(s.pv_done, t + 1)
                after(act, s.o_done, t)
                act.activation(at_hi[:], pb[3][:], ACT.Copy).then_inc(s.at_hi_done, 1)

            def step(g, j, first=False, last=False):
                t = 8 * g + j
                n = t + 4
                exps(g, j)
                if j < 4 or not last:
                    save_q(n, 1 - j // 4, j % 4)
                if not (first and j == 0):
                    save_p(t - 1)
                if j < 4 or not last:
                    square_q(n)
                if not (first and j == 0):
                    save_attention(t - 1)
                if j == 1:
                    act.wait_ge(s.wo_dma, 16 * g + 16)
                    after(act, s.o_done, 8 * g)
                    for h in range(R):
                        act.activation(wo_hi[:, h, :], wo_raw[:, h, :], ACT.Copy).then_inc(s.wo_hi_done, 1)

            for j in range(LEAD):
                step(0, j, first=j < 2)
            with act.Fori(0, G - 1) as g:
                for j in range(LEAD, 8):
                    step(g, j)
                for j in range(LEAD):
                    step(g + 1, j)
            for j in range(LEAD, 8):
                step(G - 1, j, last=True)
            save_p(G * B - 1)
            save_attention(G * B - 1)

            act.wait_ge(s.o_added, G * B)

            def split_ff(first, end):
                for n in range(first, end):
                    w, e, k = FF[n]
                    act.wait_ge(ff_dma[n % 4], 16 * (n // 4 + 1))
                    act.activation((w1_hi, w2_hi)[w][e][:, k, :], ff_raw[:, n % 4, :], ACT.Copy).then_inc(s.ff_hi_done, 1)

            split_ff(0, 8)
            save_hi(1, x2_hi)
            act.wait_ge(s.g_sub, 1)
            act.activation(gt[:, 8:11, :], gt[:, 4:7, :], ACT.Exp).then_inc(s.g_exp, 1)
            split_ff(8, 16)
            for half in range(2):
                for e in range(E):
                    unit = E * half + e
                    for m in range(KT):
                        n = KT * unit + m
                        act.wait_ge(s.pre_done, n + 1)
                        after(act, s.hid_lo_done, n - 1)
                        func = (ACT.Tanh, ACT.Gelu, ACT.Silu)[e]
                        act.activation(hid[:, m % 2, :], pb[m % 2][:], func, bias=b1_sb[:, e, m:m + 1]).then_inc(s.act_done, 1)
                        act.wait_ge(s.act_done, n + 1)
                        after(act, s.y_done, 4 * unit)
                        act.activation(hid_hi[:, m, :], hid[:, m % 2, :], ACT.Copy).then_inc(s.hid_hi_done, 1)
                    if unit == 0:
                        split_ff(16, 24)

        @block.vector
        def _(dve):
            link = Chain(dve, s.dve_link)
            for n in range(16):
                w, k, half = n // 8, n // 2 % 4, n % 2
                dve.wait_ge(s.kv_hi_done, n + 1)
                cols_ = bass.ts(half, 512)
                dve.tensor_tensor(wkv_lo[:, w, k, cols_], kv_raw[:, n % 4, :], wkv_hi[:, w, k, cols_],
                                  ALU.subtract).then_inc(s.kv_lo_done, 1)
            dve.wait_ge(s.consts, 1)
            dve.wait_ge(s.const_dma, 16 * N_CONST_DMA)
            link(dve.scalar_tensor_tensor(out=wqk[:], in0=qn_b[:], scalar=HEAD_SCALE, in1=kn_b[:],
                                          op0=ALU.mult, op1=ALU.mult))
            dve.wait_ge(s.x_dma, 16)

            def spread(ap):
                return ap.unsqueeze(2).to_broadcast([P, CG, GL, B])

            def chunk(turn, u):
                i = 2 * turn + u
                dve.wait_ge(s.ctx_hi_done, i + 1)
                dve.tensor_tensor(ctx_lo[:], ctx_raw[:, u, :], ctx_hi[:], ALU.subtract).then_inc(s.ctx_lo_done, 1)
                dve.wait_ge(s.a_scores, i + 1)
                link(dve.tensor_tensor(masked[:], pb[0][:].rearrange("p (g n) -> p g n", g=CG),
                                       blockmask[:].unsqueeze(1).to_broadcast([P, CG, P]), ALU.mult))
                ins = dve.tensor_reduce(sc[:], masked[:].rearrange("p g (l m) -> p g m l", m=B), AX, ALU.add)
                ins.then_inc(s.a_extracted, 1)
                dve.wait_ge(s.a_extracted, i + 1)
                link(dve.tensor_reduce(sc_max[:], sc[:], AX, ALU.max))
                dve.tensor_tensor(sc_sub[:], sc[:], sc_max[:].unsqueeze(2).to_broadcast([P, CG, B]),
                                  ALU.subtract).then_inc(s.a_sub, 1)
                dve.wait_ge(s.a_exp, i + 1)
                link(dve.tensor_reduce(sc_sum[:], sc_exp[:], AX, ALU.add))
                link(dve.reciprocal(sc_rec[:], sc_sum[:]))
                link(dve.tensor_tensor(sc_p[:], sc_exp[:], sc_rec[:].unsqueeze(2).to_broadcast([P, CG, B]), ALU.mult))
                after(dve, s.a_turned, i)
                dve.tensor_tensor(block_p[:].rearrange("p g (l m) -> p g l m", m=B), spread(sc_p[:]),
                                  blockmask[:].rearrange("p (l m) -> p l m", m=B).unsqueeze(1).to_broadcast([P, CG, GL, B]),
                                  ALU.mult).then_inc(s.a_probs, 1)
                dve.wait_ge(s.k_saved_raw, i + 1)
                dve.tensor_scalar(k_ms[:], k_ss[:], 1.0 / P, EPS, ALU.mult, ALU.add).then_inc(s.k_mean, 1)
                dve.wait_ge(s.k_rsqrt, i + 1)
                after(dve, s.k_turned, 2 * i)
                for c in range(G):
                    ins = dve.scalar_tensor_tensor(out=k_n[:, c, :], in0=k_raw[:, c, :], scalar=k_rstd[:, c:c + 1],
                                                   in1=wqk[:], op0=ALU.mult, op1=ALU.mult)
                ins.then_inc(s.k_normed, 1)
                dve.wait_ge(s.a_msg, i + 1)
                xs = x1[:, :, bass.ds(i * CL, CL)]
                dve.scalar_tensor_tensor(out=xs, in0=xs, scalar=2.0, in1=pb[2][:].rearrange("p (l n) -> p n l", n=B),
                                         op0=ALU.mult, op1=ALU.add).then_inc(s.a_added, 1)

            chunk(0, 0)
            chunk(0, 1)
            with dve.Fori(1, CH // 2) as turn:
                link.turn(turn - 1, 2 * 5)
                chunk(turn, 0)
                chunk(turn, 1)
            link.leave(CH // 2 - 1)
            dve.wait_ge(s.a_added, CH)

            def layer_norm(n):
                for b in range(B):
                    ins = dve.bn_stats(bn[:, b, :], x1[:, b, :])
                link(ins)
                for b in range(B):
                    ins = dve.bn_aggr(mv[:, b, :], bn[:, b, :])
                link(ins)
                dve.tensor_scalar(ve[:], mv[:, :, 1], EPS, None, ALU.add).then_inc(s.ln_var, 1)
                dve.wait_ge(s.ln_rstd, n + 1)
                for b in range(B):
                    dve.tensor_scalar(x1[:, b, :], x1[:, b, :], mv[:, b, 0:1], rstd[:, b:b + 1],
                                      ALU.subtract, ALU.mult).then_inc(s.ln_out, 1)

            def save_lo(n, hi, lo):
                for b in range(B):
                    dve.wait_ge(s.x_hi_done, B * n + b + 1)
                    cols_ = bass.ts(b, P)
                    dve.tensor_tensor(lo[:, :, cols_], pb[b % 2][:].rearrange("p (k t) -> p k t", k=KT),
                                      hi[:, :, cols_], ALU.subtract).then_inc(s.x_lo_done, 1)

            layer_norm(0)
            save_lo(0, x_hi, x_lo)

            def mean_q(n):
                dve.wait_ge(s.q_summed, n + 1)
                after(dve, s.q_rsqrt, n)
                dve.tensor_scalar(q_ms[:], pb[5][:, 0:4], 1.0 / P, EPS, ALU.mult, ALU.add).then_inc(s.q_mean, 1)

            for h in range(R):
                mean_q(h)

            def scores(g, j):
                t, half = 8 * g + j, j // 4
                dve.wait_ge(s.s_done, t + 1)
                dve.wait_ge(s.q_rsqrt, 8 * g + 4 + 4 * half)
                for h in range(R):
                    ins = dve.scalar_tensor_tensor(out=sx[:, j % 2, h, :], in0=pb[0][:, bass.ts(h, P)],
                                                   scalar=q_rstd[:, half, h, j % 4:j % 4 + 1], in1=mask_sb[:],
                                                   op0=ALU.mult, op1=ALU.add)
                ins.then_inc(s.s_masked, 1)
                dve.wait_ge(s.s_masked, t + 1)
                dve.tensor_reduce(neg_max[:], sx[:, j % 2], AX, ALU.max, negate=True).then_inc(s.s_max, 1)

            def normalise(g, j):
                t = 8 * g + j
                dve.wait_ge(s.s_exp, t + 1)
                dve.reciprocal(rsum[:], esum[:]).then_inc(s.s_rsum, 1)
                dve.wait_ge(s.s_rsum, t + 1)
                after(dve, s.p_turned, t - 1)
                dve.tensor_tensor(pr[:, j % 2], sx[:, j % 2], rsum[:].unsqueeze(2).to_broadcast([P, R, P]),
                                  ALU.mult).then_inc(s.p_done, 1)

            def add_o(t, b):
                dve.wait_ge(s.o_done, t + 1)
                dve.tensor_tensor(x1[:, b, :], x1[:, b, :], pb[4][:], ALU.add).then_inc(s.o_added, 1)

            def save_attention_lo(t):
                dve.wait_ge(s.at_hi_done, t + 1)
                dve.tensor_tensor(at_lo[:], pb[3][:].rearrange("p (h t) -> p h t", h=R), at_hi[:],
                                  ALU.subtract).then_inc(s.at_lo_done, 1)

            def step(g, j, first=False, last=False):
                t = 8 * g + j
                scores(g, j)
                normalise(g, j)
                if not first:
                    add_o(t - 2, (j - 2) % 8)
                if not (first and j == 0):
                    save_attention_lo(t - 1)
                if j == 1:
                    for h in range(R):
                        dve.wait_ge(s.wo_hi_done, 4 * g + h + 1)
                        dve.tensor_tensor(wo_lo[:, h, :], wo_raw[:, h, :], wo_hi[:, h, :],
                                          ALU.subtract).then_inc(s.wo_lo_done, 1)
                if j < 4 or not last:
                    mean_q(t + 4)

            for j in range(LEAD):
                step(0, j, first=j < 2)
            with dve.Fori(0, G - 1) as g:
                for j in range(LEAD, 8):
                    step(g, j)
                for j in range(LEAD):
                    step(g + 1, j)
            for j in range(LEAD, 8):
                step(G - 1, j, last=True)
            last = G * B - 1
            add_o(last - 1, B - 2)
            save_attention_lo(last)
            add_o(last, B - 1)
            dve.wait_ge(s.o_added, G * B)

            layer_norm(1)
            dve.wait_ge(s.ln_out, 2 * B)
            for b in range(B):
                ins = dve.tensor_reduce(row_abs[:, b:b + 1], x1[:, b, :], AX, ALU.add, apply_absolute_value=True)
            ins.then_inc(s.row_sums, 1)
            save_lo(1, x2_hi, x2_lo)
            dve.wait_ge(s.gate_in, 16 * 2 * E)
            for e in range(E):
                for b in range(B):
                    link(dve.tensor_tensor_reduce(junk[:], x1[:, b, :], gw_b[:, e, :], 1.0, 0.0, ALU.mult, ALU.add,
                                                  gt[:, e, b:b + 1]))
            v = lambda n: gt[:, n, :]
            RATIO, VS, MX, SUM, T01 = 3, 12, 13, 14, 15
            dve.wait_ge(s.means, 1)
            link(dve.tensor_scalar(v(VS), pb[2][:, B:2 * B], 1e-8, None, ALU.add))
            link(dve.reciprocal(v(MX), v(VS)))
            link(dve.tensor_tensor(v(RATIO), pb[2][:, 0:B], v(MX), ALU.mult))
            for e in range(E):
                ins = dve.scalar_tensor_tensor(out=v(16 + e), in0=v(RATIO), scalar=gw_last[:, e:e + 1], in1=v(e),
                                               op0=ALU.mult, op1=ALU.add)
            link(ins)
            for e in range(E):
                ins = dve.tensor_scalar(v(19 + e), v(16 + e), gb_sb[:, e:e + 1], None, ALU.add)
            link(ins)
            by_batch = lambda a, z: gt[:, a:z, :].rearrange("p e b -> p b e")
            over_e = lambda n: v(n).unsqueeze(1).to_broadcast([P, E, B])
            link(dve.tensor_reduce(v(22), by_batch(19, 22), AX, ALU.max))
            dve.tensor_tensor(gt[:, 4:7, :], gt[:, 19:22, :], over_e(22), ALU.subtract).then_inc(s.g_sub, 1)
            dve.wait_ge(s.g_exp, 1)
            link(dve.tensor_reduce(v(SUM), by_batch(8, 11), AX, ALU.add))
            link(dve.reciprocal(v(T01), v(SUM)))
            link(dve.tensor_tensor(gt[:, 23:26, :], gt[:, 8:11, :], over_e(T01), ALU.mult))
            a, b_, c = v(23), v(24), v(25)
            dve.tensor_tensor(v(26), a, b_, ALU.is_ge)
            dve.tensor_tensor(v(27), a, c, ALU.is_ge)
            link(dve.tensor_tensor(v(28), b_, c, ALU.is_ge))
            dve.tensor_tensor(v(32), v(26), v(27), ALU.add)
            dve.tensor_tensor(v(33), v(26), v(28), ALU.subtract)
            link(dve.tensor_tensor(v(31), v(27), v(28), ALU.add))
            dve.tensor_scalar(v(29), v(32), -1.0, 2.0, ALU.mult, ALU.add)
            link(dve.tensor_scalar(v(30), v(33), 1.0, None, ALU.add))
            for i in range(2):
                link(dve.tensor_scalar(onehot[:, i], gt[:, 29:32, :], float(i), None, ALU.is_equal))
            dve.tensor_copy(row_abs[:], row_abs[:]).then_inc(s.picked, 1)
            for i in range(2):
                link(dve.tensor_tensor(gt[:, 34:37, :], onehot[:, i], gt[:, 23:26, :], ALU.mult))
                link(dve.tensor_reduce(v(37 + i), by_batch(34, 37), AX, ALU.add))
            link(dve.tensor_tensor(v(39), v(37), v(38), ALU.add))
            link(dve.tensor_scalar(v(34), v(39), 1e-8, None, ALU.add))
            link(dve.reciprocal(v(35), v(34)))
            link(dve.tensor_tensor(gt[:, 37:39, :], gt[:, 37:39, :], v(35).unsqueeze(1).to_broadcast([P, 2, B]), ALU.mult))
            dve.wait_ge(s.choice_out, 1)
            for i in range(2):
                link(dve.tensor_tensor(choice[:, i], pb[2][:, 16 + 24 * i:40 + 24 * i].rearrange("p (e b) -> p e b", e=E),
                                       v(37 + i).unsqueeze(1).to_broadcast([P, E, B]), ALU.mult))
            link(dve.tensor_tensor(coef[:], choice[:, 0], choice[:, 1], ALU.add))
            for e in range(E):
                for b in range(B):
                    ins = dve.scalar_tensor_tensor(out=x1[:, b, :], in0=b2_b[:, e, :], scalar=coef[:, e, b:b + 1],
                                                   in1=x1[:, b, :], op0=ALU.mult, op1=ALU.add)
                link(ins)
            for half in range(2):
                for e in range(E):
                    unit = E * half + e
                    for m in range(KT):
                        n = KT * unit + m
                        dve.wait_ge(s.hid_hi_done, n + 1)
                        dve.tensor_tensor(hid_lo[:, m, :], hid[:, m % 2, :], hid_hi[:, m, :],
                                          ALU.subtract).then_inc(s.hid_lo_done, 1)
                    for t in range(4):
                        b = 4 * half + t
                        dve.wait_ge(s.y_done, 4 * unit + t + 1)
                        dve.scalar_tensor_tensor(out=x1[:, b, :], in0=pb[4 + t][:], scalar=coef[:, e, b:b + 1],
                                                 in1=x1[:, b, :], op0=ALU.mult, op1=ALU.add).then_inc(s.y_added, 1)
            dve.wait_ge(s.y_added, 24)
            layer_norm(2)

        @block.tensor
        def _(pe):
            pe.wait_ge(s.consts, 1)

            def three(out_ap, pairs):
                n = 3 * len(pairs)
                i = 0
                for w_hi, w_lo, m_hi, m_lo in pairs:
                    for w, m in ((w_hi, m_hi), (w_hi, m_lo), (w_lo, m_hi)):
                        ins = pe.matmul(out_ap, w, m, start=(i == 0), stop=(i == n - 1))
                        i += 1
                return ins

            def chunk(turn, u):
                i = 2 * turn + u
                pe.wait_ge(cols_dma[u], 16 * turn + 16)
                after(pe, s.a_extracted, i)
                for c in range(CG):
                    w = cols[:, u, bass.ts(c, P)]
                    ins = pe.matmul(pb[0][:, bass.ts(c, P)], w, w, start=True, stop=True)
                ins.then_inc(s.a_scores, 1)
                pe.wait_ge(s.ctx_lo_done, i + 1)

                def project(w, half):
                    cols_ = bass.ts(half, 512)
                    return three(pb[3 + 2 * w + half][:], [
                        (ctx_hi[:, bass.ts(k, P)], ctx_lo[:, bass.ts(k, P)],
                         wkv_hi[:, w, k, cols_], wkv_lo[:, w, k, cols_]) for k in range(KT)])

                after(pe, s.k_saved_raw, i)
                project(0, 0)
                project(0, 1).then_inc(s.k_done, 1)
                after(pe, s.v_saved, 2 * i)
                project(1, 0).then_inc(s.v_done, 1)
                pe.wait_ge(s.a_probs, i + 1)
                after(pe, s.k_saved, 2 * i)
                for c in range(CG):
                    ins = pe.transpose(pb[1][:, bass.ts(c, P)], block_p[:, c, :], ident[:])
                ins.then_inc(s.a_turned, 1)
                project(1, 1).then_inc(s.v_done, 1)
                pe.wait_ge(s.a_probs_t, i + 1)
                pe.wait_ge(rows_dma[u], 16 * turn + 16)
                after(pe, s.a_added, i)
                for c in range(CG):
                    ins = pe.matmul(pb[2][:, bass.ts(c, P)], rows[:, u, bass.ts(c, P)], block_pt[:, c, :],
                                    start=True, stop=True)
                ins.then_inc(s.a_msg, 1)
                pe.wait_ge(s.k_normed, i + 1)
                for half in range(2):
                    for c in range(4):
                        ins = pe.transpose(pb[(7, 1)[half]][:, bass.ts(c, P)], k_n[:, 4 * half + c, :], ident[:])
                    ins.then_inc(s.k_turned, 1)

            pe.wait_ge(s.kv_lo_done, 16)
            chunk(0, 0)
            chunk(0, 1)
            with pe.Fori(1, CH // 2) as turn:
                chunk(turn, 0)
                chunk(turn, 1)

            def turn_x(n):
                if n == 0:
                    pe.wait_ge(s.k_saved, 2 * B)
                for b in range(B):
                    pe.wait_ge(s.ln_out, B * n + b + 1)
                    after(pe, s.x_lo_done, B * n + b - 1)
                    for k in range(KT):
                        ins = pe.transpose(pb[b % 2][:, bass.ts(k, P)], x1[:, b, bass.ts(k, P)], ident[:])
                    ins.then_inc(s.x_turned, 1)

            turn_x(0)

            def query_piece(g, n, half, h):
                pe.wait_ge(s.wq_lo_done, 4 * g + h + 1)
                pe.wait_ge(s.x_lo_done, B)
                after(pe, s.q_squared, n)
                cols_ = bass.ts(half, HALF_T)
                three(pb[2][:], [(wq_hi[:, h, k, :], wq_lo[:, h, k, :], x_hi[:, k, cols_], x_lo[:, k, cols_])
                                 for k in range(KT)]).then_inc(s.q_done, 1)

            def query_sums(n):
                pe.wait_ge(s.q_squared, n + 1)
                after(pe, s.q_mean, n)
                for c in range(4):
                    ins = pe.matmul(pb[5][:, c:c + 1], q_sq[:, bass.ts(c, P)], ones[:], start=True, stop=True)
                ins.then_inc(s.q_summed, 1)

            for h in range(R):
                query_piece(0, h, 0, h)
                query_sums(h)

            def scores(g, j):
                t, half = 8 * g + j, j // 4
                pe.wait_ge(s.q_saved, 8 * g + 4 + 4 * half)
                after(pe, s.s_masked, t)
                for h in range(R):
                    ins = pe.matmul(pb[0][:, bass.ts(h, P)], q_t[:, half, h, bass.ts(j % 4, P)],
                                    k_t[:, bass.ds(g, 1), bass.ts(j, P)].rearrange("p a t -> p (a t)"),
                                    start=True, stop=True)
                ins.then_inc(s.s_done, 1)

            def turn_p(t, parity):
                pe.wait_ge(s.p_done, t + 1)
                after(pe, s.p_saved, t)
                for h in range(R):
                    ins = pe.transpose(pb[1][:, bass.ts(h, P)], pr[:, parity, h, :], ident[:])
                ins.then_inc(s.p_turned, 1)

            def attend(t, g, b):
                pe.wait_ge(s.p_saved, t + 1)
                pe.wait_ge(s.v_ready, 2 * g + 1 + b // 4)
                after(pe, s.at_lo_done, t)
                pe.matmul(pb[3][:], v_g[:, b, :], pr_t[:].rearrange("p h t -> p (h t)"),
                          start=True, stop=True).then_inc(s.pv_done, 1)

            def project_out(t, g):
                pe.wait_ge(s.at_lo_done, t + 1)
                pe.wait_ge(s.wo_lo_done, 4 * g + 4)
                after(pe, s.o_added, t)
                three(pb[4][:], [(at_hi[:, h, :], at_lo[:, h, :], wo_hi[:, h, :], wo_lo[:, h, :])
                                 for h in range(R)]).then_inc(s.o_done, 1)

            def step(g, j, first=False, last=False):
                t = 8 * g + j
                before = g if j > 0 else g - 1
                before2 = g if j > 1 else g - 1
                scores(g, j)
                if j < 4:
                    query_piece(g, t + 4, 1, j)
                elif not last:
                    query_piece(g + 1, t + 4, 0, j - 4)
                if not (first and j == 0):
                    turn_p(t - 1, (j - 1) % 2)
                if not first:
                    project_out(t - 2, before2)
                if not (first and j == 0):
                    attend(t - 1, before, (j - 1) % 8)
                if j < 4 or not last:
                    query_sums(t + 4)

            for j in range(LEAD):
                step(0, j, first=j < 2)
            with pe.Fori(0, G - 1) as g:
                for j in range(LEAD, 8):
                    step(g, j)
                for j in range(LEAD):
                    step(g + 1, j)
            for j in range(LEAD, 8):
                step(G - 1, j, last=True)
            last = G * B - 1
            turn_p(last, 1)
            project_out(last - 1, G - 1)
            attend(last, G - 1, B - 1)
            project_out(last, G - 1)

            turn_x(1)
            pe.wait_ge(s.row_sums, 1)
            pe.matmul(pb[2][:, 0:B], text_mean[:], row_abs[:], start=True, stop=True)
            pe.matmul(pb[2][:, B:2 * B], vis_mean[:], row_abs[:], start=True, stop=True).then_inc(s.means, 1)

            def choices():
                pe.wait_ge(s.picked, 1)
                pe.matmul(pb[2][:, 16:64], row0[:], onehot[:].rearrange("p i e b -> p (i e b)"),
                          start=True, stop=True).then_inc(s.choice_out, 1)

            for half in range(2):
                for e in range(E):
                    unit = E * half + e
                    for m in range(KT):
                        n = KT * unit + m
                        pe.wait_ge(s.ff_lo_done, ff_index[0, e, KT - 1] + 1)
                        pe.wait_ge(s.x_lo_done, B + 4 * half + 4 if n else 2 * B)
                        after(pe, s.act_done, n - 1)
                        cols_ = bass.ts(half, HALF_T)
                        three(pb[m % 2][:], [(w1_hi[e][:, k, bass.ts(m, P)], w1_lo[e][:, k, bass.ts(m, P)],
                                              x2_hi[:, k, cols_], x2_lo[:, k, cols_])
                                             for k in range(KT)]).then_inc(s.pre_done, 1)
                    if unit == 0:
                        choices()
                    pe.wait_ge(s.ff_lo_done, ff_index[1, e, KT - 1] + 1)
                    after(pe, s.y_added, 4 * unit)
                    for m in range(KT):
                        pe.wait_ge(s.hid_lo_done, KT * unit + m + 1)
                        for t in range(4):
                            rows_ = bass.ts(t, P)
                            for i, (w, r) in enumerate(((hid_hi, w2_hi), (hid_hi, w2_lo), (hid_lo, w2_hi))):
                                ins = pe.matmul(pb[4 + t][:], w[:, m, rows_], r[e][:, m, :],
                                                start=(m == 0 and i == 0), stop=(m == KT - 1 and i == 2))
                            if m == KT - 1:
                                ins.then_inc(s.y_done, 1)


def kernel(**inputs):
    import numpy as np
    import concourse.bacc as bacc
    from concourse.bass_utils import run_bass_kernel_spmd as run

    a = {n: np.asarray(v) for n, v in inputs.items()}
    x = a["x"]
    wk, wv = a["L0_xattn_k_proj_w"], a["L0_xattn_v_proj_w"]
    w2t = lambda w: w.reshape(2, 512, KT, P).transpose(3, 2, 0, 1)
    arrays = {
        "x_nat": x,
        "x_cols": x.transpose(1, 2, 0).reshape(P, CH, CL * B).transpose(1, 0, 2),
        "x_rows": x.transpose(2, 0, 1).reshape(CH, CG, P, P).transpose(0, 2, 1, 3).reshape(CH, P, CG * P),
        "ctx_t": a["ctx_4096"].reshape(B, P, KT, P).transpose(0, 3, 2, 1).reshape(B, P, KT * P),
        "mask": a["mask_1x1xSxS2_ff0"].reshape(P, P),
        "wq_t": a["L0_xattn_q_proj_w"].reshape(G * R, P, KT, P).transpose(0, 3, 2, 1).reshape(G * R, P, KT * P),
        "wkv_t": np.stack([w2t(w)[:, k, half] for w in (wk, wv) for k in range(KT) for half in range(2)]),
        "wo_t": a["L0_xattn_o_proj_w"].T.reshape(G, R, P, D).transpose(0, 2, 1, 3),
        "qn_w": a["L0_xattn_q_norm_w"], "kn_w": a["L0_xattn_k_norm_w"],
        "gate_wt": a["L0_ffn_gate_w"][:D].T, "gate_last": a["L0_ffn_gate_w"][D], "gate_b": a["L0_ffn_gate_b"],
        "w1": a["L0_ffn_w1"], "b1_t": a["L0_ffn_b1"].reshape(E, KT, P).transpose(2, 0, 1),
        "w2": a["L0_ffn_w2"], "b2": a["L0_ffn_b2"],
    }
    arrays = {n: np.ascontiguousarray(v) for n, v in arrays.items()}
    nc = bacc.Bacc("TRN2", target_bir_lowering=False, num_devices=1)
    aps = [nc.dram_tensor(n, v.shape, F32, kind="ExternalInput").ap() for n, v in arrays.items()]
    out = nc.dram_tensor("out", (B, P, D), F32, kind="ExternalOutput").ap()
    build(nc, *aps, out)
    r = run(nc, [arrays], core_ids=[0])
    return r.results[0]["out"]
```

```python
from contextlib import ExitStack

import concourse.bass as bass
from concourse import mybir

F32 = mybir.dt.float32
F32R = mybir.dt.float32r
ACT = mybir.ActivationFunctionType
ALU = mybir.AluOpType
AX = mybir.AxisListType.X

P = 128
B = 8
D = 512
KT = D // P
T = B * P
HALF_T = T // 2
G = 8
R = 4
CH = 8
CG = 4
GL = 16
CL = CG * GL
E = 3
VIS = int(P * 0.3)
EPS = 1e-5
PIECE = ((1, 1), (1, 2), (1, 3), (0, 0), (0, 1), (0, 2), (0, 3), (1, 0))
SELF_SCALE = float(P) ** -0.5
HEAD_SCALE = float(P) ** -0.5


class Chain:

    def __init__(self, eng, sem):
        self.eng, self.sem, self.base, self.n = eng, sem, 0, 0

    def __call__(self, ins):
        self.n += 1
        ins.then_inc(self.sem, 1)
        self.eng.wait_ge(self.sem, self.base + self.n)

    def turn(self, turns, per):
        self.ahead, self.per = self.n, per
        self.base, self.n = self.ahead + turns * per, 0

    def leave(self, turns):
        assert self.n == self.per, (self.n, self.per)
        self.base, self.n = 0, self.ahead + turns * self.per


class Semaphores:

    def __init__(self, sem):
        self.consts = sem("consts")
        self.const_dma = sem("const_dma")
        self.kv_hi_done = sem("kv_hi_done")
        self.kv_lo_done = sem("kv_lo_done")
        self.x_dma = sem("x_dma")
        self.ctx_hi_done = sem("ctx_hi_done")
        self.ctx_lo_done = sem("ctx_lo_done")
        self.a_scores = sem("a_scores")
        self.a_extracted = sem("a_extracted")
        self.a_sub = sem("a_sub")
        self.a_exp = sem("a_exp")
        self.a_probs = sem("a_probs")
        self.a_turned = sem("a_turned")
        self.a_probs_t = sem("a_probs_t")
        self.a_msg = sem("a_msg")
        self.a_added = sem("a_added")
        self.projected = sem("projected")
        self.k_raw_done = sem("k_raw_done")
        self.k_mean = sem("k_mean")
        self.k_rsqrt = sem("k_rsqrt")
        self.k_normed = sem("k_normed")
        self.k_turned = sem("k_turned")
        self.k_saved = sem("k_saved")
        self.v_done = sem("v_done")
        self.v_saved = sem("v_saved")
        self.ln_var = sem("ln_var")
        self.ln_rstd = sem("ln_rstd")
        self.ln_out = sem("ln_out")
        self.x_turned = sem("x_turned")
        self.x_hi_done = sem("x_hi_done")
        self.x_lo_done = sem("x_lo_done")
        self.wq_hi_done = sem("wq_hi_done")
        self.wq_lo_done = sem("wq_lo_done")
        self.wo_dma = sem("wo_dma")
        self.wo_hi_done = sem("wo_hi_done")
        self.wo_lo_done = sem("wo_lo_done")
        self.wo2_hi_done = sem("wo2_hi_done")
        self.wo2_lo_done = sem("wo2_lo_done")
        self.gate_hi_done = sem("gate_hi_done")
        self.gate_lo_done = sem("gate_lo_done")
        self.q_done = sem("q_done")
        self.q_saved = sem("q_saved")
        self.q_squared = sem("q_squared")
        self.q_sq_hi_done = sem("q_sq_hi_done")
        self.q_sq_lo_done = sem("q_sq_lo_done")
        self.q_summed = sem("q_summed")
        self.q_row_saved = sem("q_row_saved")
        self.q_sums_turned = sem("q_sums_turned")
        self.q_mean = sem("q_mean")
        self.q_rsqrt = sem("q_rsqrt")
        self.s_done = sem("s_done")
        self.s_masked = sem("s_masked")
        self.s_max = sem("s_max")
        self.s_exp = sem("s_exp")
        self.s_rsum = sem("s_rsum")
        self.p_done = sem("p_done")
        self.p_turned = sem("p_turned")
        self.p_hi_done = sem("p_hi_done")
        self.p_lo_done = sem("p_lo_done")
        self.v_hi_done = sem("v_hi_done")
        self.v_lo_done = sem("v_lo_done")
        self.pv_done = sem("pv_done")
        self.at_hi_done = sem("at_hi_done")
        self.at_lo_done = sem("at_lo_done")
        self.o_done = sem("o_done")
        self.o_added = sem("o_added")
        self.ff_hi_done = sem("ff_hi_done")
        self.ff_lo_done = sem("ff_lo_done")
        self.row_sums = sem("row_sums")
        self.means = sem("means")
        self.picked = sem("picked")
        self.choice_out = sem("choice_out")
        self.pre_done = sem("pre_done")
        self.act_done = sem("act_done")
        self.hid_hi_done = sem("hid_hi_done")
        self.hid_lo_done = sem("hid_lo_done")
        self.y_done = sem("y_done")
        self.y_saved = sem("y_saved")
        self.y_added = sem("y_added")
        self.g_sub = sem("g_sub")
        self.g_exp = sem("g_exp")
        self.logits = sem("logits")
        self.b2_dma = sem("b2_dma")
        self.store = sem("store")
        self.dve_link = sem("dve_link")
        self.pool_link = sem("pool_link")
        self.kv_dma = [sem(f"kv_dma{i}") for i in range(4)]
        self.ff_dma = [sem(f"ff_dma{i}") for i in range(4)]
        self.wq_dma = [sem(f"wq_dma{i}") for i in range(2)]
        self.cols_dma = [sem(f"cols_dma{i}") for i in range(2)]
        self.rows_dma = [sem(f"rows_dma{i}") for i in range(2)]
        self.ctx_dma = [sem(f"ctx_dma{i}") for i in range(2)]


def after(eng, sem, value):
    if not isinstance(value, int) or value > 0:
        eng.wait_ge(sem, value)


def build(nc, x_nat, x_cols, x_rows, ctx_t, mask, wq_t, wkv_t, wo_t, qn_w, kn_w,
          gate_wp, gate_last, gate_b, w1, b1_t, w2, b2, out):
    with ExitStack() as stack:
        cur = [(nc.sbuf_base + 63) // 64 * 64]
        at = {}

        def sb(name, shape, dt=F32):
            size = 4
            for n in shape[1:]:
                size *= n
            at[name] = cur[0]
            t = nc.alloc_sbuf_tensor_at(name, shape, dt, offset=cur[0])
            cur[0] += (size + 31) // 32 * 32
            assert cur[0] <= nc.sbuf_usable_end, (name, cur[0])
            return t

        def bank(name):
            return stack.enter_context(nc.psum_tensor(name, [P, 512], F32))

        ident = sb("ident", [P, P])
        blockmask = sb("blockmask", [P, P])
        mask_sb = sb("mask_sb", [P, P])
        text_mean = sb("text_mean", [P, P])
        vis_mean = sb("vis_mean", [P, P])
        row0 = sb("row0", [P, P])
        head_row = sb("head_row", [P, R, P], F32R)
        ones = sb("ones", [P, 1])
        neghalf = sb("neghalf", [P, 16])
        qn_b = sb("qn_b", [P, P])
        kn_b = sb("kn_b", [P, P])
        bn = sb("bn", [P, B, 6])
        mv = sb("mv", [P, B, 2])
        ve = sb("ve", [P, B])
        rstd = sb("rstd", [P, B])
        b1_sb = sb("b1_sb", [P, E, KT])
        gate_raw = sb("gate_raw", [P, KT, E + 1])
        gate_hi = sb("gate_hi", [P, KT, E + 1], F32R)
        gate_lo = sb("gate_lo", [P, KT, E + 1], F32R)
        gw_last = sb("gw_last", [P, E])
        gb_sb = sb("gb_sb", [P, E])
        q_ms = sb("q_ms", [P, 16])
        q_rstd = sb("q_rstd", [P, 2, 16])
        row_abs = sb("row_abs", [P, B])
        neg_max = sb("neg_max", [P, R])
        esum = sb("esum", [P, R])
        rsum = sb("rsum", [P, R])
        x1 = sb("x1", [P, B, D])
        wq_raw = sb("wq_raw", [P, 2, KT * P])
        wo_raw = sb("wo_raw", [P, R, D])
        kv_raw = ff_raw = wo_raw
        wqk = qn_b
        wq_hi = sb("wq_hi", [P, R, KT, P], F32R)
        wq_lo = sb("wq_lo", [P, R, KT, P], F32R)
        k_t = sb("k_t", [P, G, T])
        v_all = sb("v_all", [P, B, G * P])
        at_ab = cur[0]
        wk_hi = sb("wk_hi", [P, KT, G * P], F32R)
        wk_lo = sb("wk_lo", [P, KT, G * P], F32R)
        wv_hi = sb("wv_hi", [P, KT, G * P], F32R)
        wv_lo = sb("wv_lo", [P, KT, G * P], F32R)
        cols = sb("cols", [P, 2, 512])
        rows = sb("rows", [P, 2, 512])
        ctx_raw = sb("ctx_raw", [P, 2, 512])
        ctx_hi = sb("ctx_hi", [P, 2, 512], F32R)
        ctx_lo = sb("ctx_lo", [P, 2, 512], F32R)
        block_p = sb("block_p", [P, CG, P])
        block_pt = sb("block_pt", [P, CG, P])
        sc = sb("sc", [P, CG, B])
        sc_max = sb("sc_max", [P, CG])
        sc_sub = sb("sc_sub", [P, CG, B])
        sc_exp = sb("sc_exp", [P, CG, B])
        sc_sum = sb("sc_sum", [P, CG])
        sc_rec = sb("sc_rec", [P, CG])
        sc_p = sb("sc_p", [P, CG, B])
        k_raw = sb("k_raw", [P, G, P])
        k_ss = sb("k_ss", [P, G])
        k_ms = sb("k_ms", [P, G])
        k_rstd = sb("k_rstd", [P, G])
        cur[0] = at_ab
        x_hi = sb("x_hi", [P, KT, T], F32R)
        x_lo = sb("x_lo", [P, KT, T], F32R)
        q_t = sb("q_t", [P, 2, R, HALF_T])
        wo_hi = sb("wo_hi", [P, R, D], F32R)
        wo_lo = sb("wo_lo", [P, R, D], F32R)
        sx = sb("sx", [P, R, P])
        pr = sb("pr", [P, R, P])
        at_rest = cur[0]
        q_sq_hi = sb("q_sq_hi", [P, HALF_T], F32R)
        q_sq_lo = sb("q_sq_lo", [P, HALF_T], F32R)
        q_row = sb("q_row", [P, HALF_T])
        v_hi = sb("v_hi", [P, B, P], F32R)
        v_lo = sb("v_lo", [P, B, P], F32R)
        pt_hi = sb("pt_hi", [P, R, P], F32R)
        pt_lo = sb("pt_lo", [P, R, P], F32R)
        at_hi = sb("at_hi", [P, R, P], F32R)
        at_lo = sb("at_lo", [P, R, P], F32R)
        w1_hi, w1_lo, w2_hi, w2_lo = [None] * E, [None] * E, [None] * E, [None] * E

        def place(where, e, hi, lo, name):
            cur[0] = where
            hi[e] = sb(f"{name}_hi{e}", [P, KT, D], F32R)
            lo[e] = sb(f"{name}_lo{e}", [P, KT, D], F32R)
            return cur[0]

        place(place(at["x_hi"], 0, w1_hi, w1_lo, "w1"), 0, w2_hi, w2_lo, "w2")
        place(at["wq_hi"], 1, w1_hi, w1_lo, "w1")
        place(place(at["k_t"], 1, w2_hi, w2_lo, "w2"), 2, w1_hi, w1_lo, "w1")
        place(at["wo_hi"], 2, w2_hi, w2_lo, "w2")
        cur[0] = at["v_all"]
        x2_hi = sb("x2_hi", [P, KT, T], F32R)
        x2_lo = sb("x2_lo", [P, KT, T], F32R)
        cur[0] = at["q_t"]
        hid_hi = sb("hid_hi", [P, KT, HALF_T], F32R)
        hid_lo = sb("hid_lo", [P, KT, HALF_T], F32R)
        cur[0] = at["sx"]
        hid = sb("hid", [P, 2, HALF_T])
        cur[0] = at_rest
        junk = sb("junk", [P, D])
        b2_b = sb("b2_b", [P, E, D])
        y_raw = sb("y_raw", [P, 4, D])
        gt = sb("gt", [P, 40, B])
        onehot = sb("onehot", [P, 2, E, B])
        choice = sb("choice", [P, 2, E, B])
        coef = sb("coef", [P, E, B])

        pb = [bank(f"bank{i}") for i in range(8)]
        Y_BANKS = (3, 4, 5, 7)
        s = Semaphores(lambda name: stack.enter_context(nc.semaphore(name)))
        N_CONST_DMA = 7
        block = stack.enter_context(nc.Block())

        FF = [(w, e, k) for e in range(E) for w in (0, 1) for k in range(KT)]
        ff_index = {wek: n for n, wek in enumerate(FF)}
        LAST = G * B - 1

        @block.sync
        def _(sp):
            flat = lambda a: a.rearrange("a p n -> p (a n)")

            def load_kv(n):
                after(sp, s.kv_lo_done, n - 3)
                sp.dma_start(kv_raw[:, n % 4, :], wkv_t[n]).then_inc(s.kv_dma[n % 4], 16)

            sp.dma_start(cols[:, 0, :], x_cols[0]).then_inc(s.cols_dma[0], 16)
            for n in range(4):
                load_kv(n)
            sp.dma_start(ctx_raw[:, 0, :], ctx_t[0]).then_inc(s.ctx_dma[0], 16)
            one = lambda a: a.rearrange("(a d) -> a d", a=1)
            for dst, src in (
                (qn_b[:], one(qn_w).to_broadcast([P, P])), (kn_b[:], one(kn_w).to_broadcast([P, P])),
                (mask_sb[:], mask), (b1_sb[:], b1_t), (gate_raw[:], gate_wp),
                (gw_last[:], one(gate_last).to_broadcast([P, E])), (gb_sb[:], one(gate_b).to_broadcast([P, E])),
            ):
                sp.dma_start(dst, src).then_inc(s.const_dma, 16)
            for n in range(4, 8):
                load_kv(n)
            sp.dma_start(rows[:, 0, :], x_rows[0]).then_inc(s.rows_dma[0], 16)
            sp.dma_start(cols[:, 1, :], x_cols[1]).then_inc(s.cols_dma[1], 16)
            sp.dma_start(ctx_raw[:, 1, :], ctx_t[1]).then_inc(s.ctx_dma[1], 16)
            for n in range(8, 12):
                load_kv(n)
            sp.dma_start(x1[:], x_nat.rearrange("b c l -> c b l")).then_inc(s.x_dma, 16)
            for n in range(12, 16):
                load_kv(n)
            sp.dma_start(rows[:, 1, :], x_rows[1]).then_inc(s.rows_dma[1], 16)
            for m in range(2):
                sp.dma_start(wq_raw[:, m, :], wq_t[m]).then_inc(s.wq_dma[m], 16)
            with sp.Fori(1, CH // 2) as turn:
                for u in range(2):
                    i = 2 * turn + u
                    sp.wait_ge(s.ctx_lo_done, i - 1)
                    sp.dma_start(ctx_raw[:, u, :], flat(ctx_t[bass.ds(i, 1)])).then_inc(s.ctx_dma[u], 16)
                    sp.wait_ge(s.a_scores, i - 1)
                    sp.dma_start(cols[:, u, :], flat(x_cols[bass.ds(i, 1)])).then_inc(s.cols_dma[u], 16)
                    sp.wait_ge(s.a_msg, i - 1)
                    sp.dma_start(rows[:, u, :], flat(x_rows[bass.ds(i, 1)])).then_inc(s.rows_dma[u], 16)
            sp.wait_ge(s.kv_lo_done, 16)
            sp.dma_start(wo_raw[:], wo_t[0]).then_inc(s.wo_dma, 16)
            for m in range(2, 4):
                sp.wait_ge(s.wq_lo_done, m - 1)
                sp.dma_start(wq_raw[:, m % 2, :], wq_t[m]).then_inc(s.wq_dma[m % 2], 16)
            with sp.Fori(0, G - 1) as g:
                for h in range(R):
                    m = 4 * g + 4 + h
                    sp.wait_ge(s.wq_lo_done, m - 1)
                    sp.dma_start(wq_raw[:, h % 2, :], flat(wq_t[bass.ds(m, 1)])).then_inc(s.wq_dma[h % 2], 16)
                    if h == 1:
                        sp.wait_ge(s.wo_lo_done, 2 * g + 2)
                        sp.wait_ge(s.wo2_lo_done, 2 * g + 2)
                        sp.dma_start(wo_raw[:], wo_t[bass.ds(g + 1, 1)].rearrange("a p h n -> p (a h) n")).then_inc(s.wo_dma, 16)
            sp.wait_ge(s.wo_lo_done, 2 * G)
            sp.wait_ge(s.wo2_lo_done, 2 * G)

            def load_ff(first, end):
                for n in range(first, end):
                    w, e, k = FF[n]
                    after(sp, s.ff_lo_done, n - 3)
                    sp.dma_start(ff_raw[:, n % 4, :], (w1, w2)[w][e, k * P:(k + 1) * P, :]).then_inc(s.ff_dma[n % 4], 16)

            load_ff(0, 12)
            sp.wait_ge(s.at_lo_done, LAST + 1)
            sp.wait_ge(s.o_done, LAST + 1)
            for e in range(E):
                sp.dma_start(b2_b[:, e, :], b2[e:e + 1, :].to_broadcast([P, D])).then_inc(s.b2_dma, 16)
            load_ff(12, 24)
            for b in range(B):
                sp.wait_ge(s.ln_out, 2 * B + b + 1)
                sp.dma_start(out[b], x1[:, b, :]).then_inc(s.store, 16)
            sp.wait_ge(s.store, 16 * B)

        @block.gpsimd
        def _(pool):
            link = Chain(pool, s.pool_link)

            def keep(t, compare, base, pattern, per_partition):
                link(pool.affine_select(out=t, in_=t, compare_op=compare, fill=0.0, base=base,
                                        pattern=pattern, channel_multiplier=per_partition))

            link(pool.memset(ident[:], 1.0))
            keep(ident[:], ALU.is_equal, 0, [[-1, P]], 1)
            bm = blockmask[:].rearrange("p (l m) -> p l m", m=B)
            link(pool.memset(blockmask[:], 1.0))
            keep(bm, ALU.is_ge, 0, [[-B, GL], [0, B]], 1)
            keep(bm, ALU.is_ge, B - 1, [[B, GL], [0, B]], -1)
            pool.memset(ones[:], 1.0)
            pool.memset(neghalf[:], -0.5).then_inc(s.consts, 1)
            pool.wait_ge(s.consts, 1)

            def rsqrt(dst, src, n):
                return pool.tensor_tensor(dst, src, neghalf[:, 0:n], ALU.pow)

            def split(hi, lo, raw, hi_done, lo_done, n):
                shape = list(raw.shape)
                unit = ones[:] if len(shape) == 2 else ones[:].unsqueeze(1)
                pool.tensor_tensor(hi, raw, unit.to_broadcast(shape), ALU.mult).then_inc(hi_done, 1)
                pool.wait_ge(hi_done, n + 1)
                pool.tensor_tensor(lo, raw, hi, ALU.subtract).then_inc(lo_done, 1)

            def split_ctx(turn, u):
                c = 2 * turn + u
                pool.wait_ge(s.ctx_dma[u], 16 * turn + 16)
                after(pool, s.v_done, 2 * (c - 1))
                split(ctx_hi[:, u, :], ctx_lo[:, u, :], ctx_raw[:, u, :], s.ctx_hi_done, s.ctx_lo_done, c)

            split_ctx(0, 0)
            pool.wait_ge(s.ctx_dma[1], 16)
            split(ctx_hi[:, 1, :], ctx_lo[:, 1, :], ctx_raw[:, 1, :], s.ctx_hi_done, s.ctx_lo_done, 1)
            pool.affine_select(out=head_row[:], in_=ones[:].unsqueeze(1).to_broadcast([P, R, P]), compare_op=ALU.is_equal,
                               fill=0.0, base=0, pattern=[[1, R], [-1, P]], channel_multiplier=0).then_inc(s.consts, 1)
            link(pool.memset(text_mean[:], 1.0 / ((P - VIS) * D)))
            keep(text_mean[:], ALU.is_ge, -VIS, [[0, P]], 1)
            link(pool.memset(vis_mean[:], 1.0 / (VIS * D)))
            keep(vis_mean[:], ALU.is_ge, VIS - 1, [[0, P]], -1)
            link(pool.memset(row0[:], 1.0))
            pool.affine_select(out=row0[:], in_=row0[:], compare_op=ALU.is_ge, fill=0.0, base=0,
                               pattern=[[0, P]], channel_multiplier=-1).then_inc(s.consts, 1)

            def keys_rsqrt(i):
                pool.wait_ge(s.k_mean, i + 1)
                rsqrt(k_rstd[:], k_ms[:], G).then_inc(s.k_rsqrt, 1)

            with pool.Fori(0, CH // 2 - 1) as turn:
                for u in range(2):
                    keys_rsqrt(2 * turn + u)
                    split_ctx(turn + 1, u)
            keys_rsqrt(B - 2)

            def split_wq(g, h, with_v=None):
                raw = wq_raw[:, h % 2, :].rearrange("p (k d) -> p k d", k=KT)
                unit = ones[:].unsqueeze(1)
                pool.wait_ge(s.wq_dma[h % 2], 32 * g + 16 * (h // 2 + 1))
                pool.tensor_tensor(wq_hi[:, h], raw, unit.to_broadcast([P, KT, P]), ALU.mult).then_inc(s.wq_hi_done, 1)
                if with_v:
                    vg, half = with_v
                    b = slice(4 * half, 4 * half + 4)
                    v_raw = v_all[:, b, bass.ds(vg * P, P)]
                    pool.tensor_tensor(v_hi[:, b, :], v_raw, unit.to_broadcast([P, 4, P]), ALU.mult).then_inc(s.v_hi_done, 1)
                    pool.wait_ge(s.v_hi_done, 2 * vg + half + 1)
                pool.wait_ge(s.wq_hi_done, 4 * g + h + 1)
                pool.tensor_tensor(wq_lo[:, h], raw, wq_hi[:, h], ALU.subtract).then_inc(s.wq_lo_done, 1)
                if with_v:
                    pool.tensor_tensor(v_lo[:, b, :], v_raw, v_hi[:, b, :], ALU.subtract).then_inc(s.v_lo_done, 1)

            for h in range(3):
                split_wq(0, h)
            for half in range(2):
                pool.wait_ge(s.ln_var, half + 1)
                b = slice(4 * half, 4 * half + 4)
                rsqrt(rstd[:, b], ve[:, b], 4).then_inc(s.ln_rstd, 1)
            keys_rsqrt(B - 1)
            split_wq(0, 3)

            def split_v(g, half):
                b = slice(4 * half, 4 * half + 4)
                split(v_hi[:, b, :], v_lo[:, b, :], v_all[:, b, bass.ds(g * P, P)], s.v_hi_done, s.v_lo_done, 2 * g + half)

            def half_rsqrt(hh, half):
                pool.wait_ge(s.q_mean, hh + 1)
                rsqrt(q_rstd[:, half, :], q_ms[:], 16).then_inc(s.q_rsqrt, 1)

            pool.wait_ge(s.v_saved, 2 * B)
            pool.wait_ge(s.k_saved, 2 * B)
            split_v(0, 0)
            half_rsqrt(0, 0)

            def split_wo(g):
                pool.wait_ge(s.wo_dma, 16 * g + 16)
                after(pool, s.o_done, 8 * g)
                for h in (2, 3):
                    split(wo_hi[:, h, :], wo_lo[:, h, :], wo_raw[:, h, :], s.wo2_hi_done, s.wo2_lo_done, 2 * g + h - 2)

            def step(g, j, last=False):
                if j == 0 and not last:
                    pool.wait_ge(s.q_done, 8 * g + 5)
                    split_wq(g + 1, 0)
                if j == 1:
                    split_wo(g)
                if j == 2:
                    after(pool, s.pv_done, 8 * g)
                    if last:
                        split_v(g, 1)
                    else:
                        pool.wait_ge(s.q_done, 8 * g + 6)
                        split_wq(g + 1, 1, with_v=(g, 1))
                if j == 3:
                    half_rsqrt(2 * g + 1, 1)
                if j == 4 and not last:
                    pool.wait_ge(s.q_done, 8 * g + 7)
                    split_wq(g + 1, 2)
                if j == 5 and not last:
                    pool.wait_ge(s.pv_done, 8 * g + 4)
                    pool.wait_ge(s.q_done, 8 * g + 8)
                    split_wq(g + 1, 3, with_v=(g + 1, 0))
                if j == 7 and not last:
                    half_rsqrt(2 * g + 2, 0)

            for j in range(8):
                step(0, j)
            with pool.Fori(1, G - 1) as g:
                for j in range(8):
                    step(g, j)
            for j in range(4):
                step(G - 1, j, last=True)

            def ln_rsqrt(n, b):
                pool.wait_ge(s.ln_var, n)
                rsqrt(rstd[:, b:b + 1], ve[:, b:b + 1], 1).then_inc(s.ln_rstd, 1)

            def split_ff(first, end):
                for n in range(first, end):
                    w, e, k = FF[n]
                    hi, lo = ((w1_hi, w1_lo), (w2_hi, w2_lo))[w]
                    pool.wait_ge(s.ff_dma[n % 4], 16 * (n // 4 + 1))
                    split(hi[e][:, k, :], lo[e][:, k, :], ff_raw[:, n % 4, :], s.ff_hi_done, s.ff_lo_done, n)

            pool.wait_ge(s.q_done, 8 * G)
            for b in range(6):
                split_ff(2 * b, 2 * b + 2)
                ln_rsqrt(3 + b, b)
            pool.wait_ge(s.s_done, LAST + 1)
            split_ff(12, 14)
            ln_rsqrt(9, 6)
            split_ff(14, 16)
            ln_rsqrt(10, 7)
            split_ff(16, 20)
            pool.wait_ge(s.o_done, LAST + 1)
            split_ff(20, 24)
            for b in range(B):
                ln_rsqrt(11 + b, b)

        @block.scalar
        def _(act):
            def copy(dst, src):
                return act.activation(dst, src, ACT.Copy)

            def split_kv(first, end):
                for n in range(first, end):
                    act.wait_ge(s.kv_dma[n % 4], 16 * (n // 4 + 1))
                    hi = (wk_hi, wv_hi)[n // 8]
                    copy(hi[:, n % 4, bass.ts(n // 4 % 2, 512)], kv_raw[:, n % 4, :]).then_inc(s.kv_hi_done, 1)

            def save_keys(i, half):
                act.wait_ge(s.k_turned, 2 * i + half + 1)
                copy(k_t[:, 4 * half:4 * half + 4, bass.ds(i * P, P)], pb[5][:]).then_inc(s.k_saved, 1)

            def save_values(i):
                for half in range(2):
                    act.wait_ge(s.v_done, 2 * i + half + 1)
                    dst = v_all[:, bass.ds(i, 1), bass.ts(half, 512)].rearrange("p a n -> p (a n)")
                    copy(dst, pb[6 + half][:]).then_inc(s.v_saved, 1)

            def chunk(turn, u, first=False):
                i = 2 * turn + u
                act.wait_ge(s.a_sub, i + 1)
                act.activation(sc_exp[:], sc_sub[:], ACT.Exp, scale=SELF_SCALE).then_inc(s.a_exp, 1)
                if not first:
                    save_values(i - 1)
                act.wait_ge(s.a_turned, i + 1)
                after(act, s.a_msg, i)
                copy(block_pt[:], pb[1][:]).then_inc(s.a_probs_t, 1)
                if not first:
                    for half in range(2):
                        save_keys(i - 1, half)
                act.wait_ge(s.projected, i + 1)
                for half in range(2):
                    copy(k_raw[:, 4 * half:4 * half + 4, :], pb[3 + half][:]).then_inc(s.k_raw_done, 1)
                act.wait_ge(s.k_raw_done, 3 * i + 2)
                for half in range(2):
                    for c in range(4):
                        bank_ = pb[3 + half][:, bass.ts(c, P)]
                        ins = act.activation(bank_, bank_, ACT.Square, accum_out=k_ss[:, 4 * half + c:4 * half + c + 1])
                ins.then_inc(s.k_raw_done, 1)

            split_kv(0, 8)
            chunk(0, 0, first=True)
            split_kv(8, 16)
            chunk(0, 1)
            with act.Fori(1, CH // 2) as turn:
                chunk(turn, 0)
                chunk(turn, 1)

            def save_hi(n, b, hi, bank_):
                act.wait_ge(s.x_turned, B * n + b + 1)
                copy(hi[:, :, bass.ts(b, P)], pb[bank_][:].rearrange("p (k t) -> p k t", k=KT)).then_inc(s.x_hi_done, 1)

            save_values(B - 1)
            for b in range(4):
                save_hi(0, b, x_hi, b % 2)

            def save_q(n, half, h, parity):
                act.wait_ge(s.q_done, n + 1)
                copy(q_t[:, half, h, :], pb[(2, 6)[parity]][:]).then_inc(s.q_saved, 1)

            def square_q(n, parity):
                bank_ = pb[(2, 6)[parity]][:]
                act.wait_ge(s.q_saved, n + 1)
                act.activation(bank_, bank_, ACT.Square).then_inc(s.q_squared, 1)
                act.wait_ge(s.q_squared, n + 1)
                after(act, s.q_summed, n)
                copy(q_sq_hi[:], bank_).then_inc(s.q_sq_hi_done, 1)

            def save_sums(hh):
                act.wait_ge(s.q_summed, 4 * hh + 4)
                after(act, s.q_sums_turned, hh)
                copy(q_row[:], pb[5][:]).then_inc(s.q_row_saved, 1)

            save_q(0, 0, 0, 0)
            save_hi(0, 4, x_hi, 0)
            square_q(0, 0)
            save_hi(0, 5, x_hi, 1)
            save_keys(B - 1, 0)
            save_q(1, 0, 1, 1)
            save_hi(0, 6, x_hi, 0)
            save_hi(0, 7, x_hi, 1)
            save_keys(B - 1, 1)
            square_q(1, 1)
            for n in range(2, 5):
                save_q(n, n // 4, n % 4, n % 2)
                square_q(n, n % 2)
            save_sums(0)
            act.wait_ge(s.const_dma, 16 * N_CONST_DMA)
            copy(gate_hi[:], gate_raw[:]).then_inc(s.gate_hi_done, 1)

            def exps(t):
                act.wait_ge(s.s_max, t + 1)
                for h in range(R):
                    ins = act.activation(sx[:, h, :], sx[:, h, :], ACT.Exp, bias=neg_max[:, h:h + 1],
                                         accum_out=esum[:, h:h + 1])
                ins.then_inc(s.s_exp, 1)

            def save_p(t):
                act.wait_ge(s.p_turned, t + 1)
                after(act, s.pv_done, t)
                copy(pt_hi[:], pb[1][:]).then_inc(s.p_hi_done, 1)

            def save_attention(t):
                act.wait_ge(s.pv_done, t + 1)
                after(act, s.o_done, t)
                copy(at_hi[:], pb[3][:]).then_inc(s.at_hi_done, 1)

            def step(g, j, first=False, last=False):
                t = 8 * g + j
                n = t + 5
                piece = j < 3 or not last
                exps(t)
                if piece:
                    save_q(n, *PIECE[j], (j + 1) % 2)
                if not (first and j < 1):
                    save_p(t - 1)
                if piece:
                    square_q(n, (j + 1) % 2)
                if not (first and j < 1):
                    save_attention(t - 1)
                if j == 2 or j == 6 and not last:
                    save_sums(2 * g + 1 + j // 4)
                if j == 1:
                    act.wait_ge(s.wo_dma, 16 * g + 16)
                    after(act, s.o_done, 8 * g)
                    for h in range(2):
                        copy(wo_hi[:, h, :], wo_raw[:, h, :]).then_inc(s.wo_hi_done, 1)

            for j in range(8):
                step(0, j, first=True)
            with act.Fori(1, G - 1) as g:
                for j in range(8):
                    step(g, j)
            for j in range(3):
                step(G - 1, j, last=True)

            def row_sum(b):
                act.wait_ge(s.ln_out, B + b + 1)
                after(act, s.row_sums, b)
                act.activation(junk[:], x1[:, b, :], ACT.Abs, accum_out=row_abs[:, b:b + 1]).then_inc(s.row_sums, 1)

            def save_x2(b):
                save_hi(1, b, x2_hi, (2, 6)[b % 2])

            act.wait_ge(s.q_summed, 8 * G)
            act.wait_ge(s.v_lo_done, 2 * G)
            for j in range(3, 8):
                save_p(LAST - 8 + j)
                exps(LAST - 7 + j)
                save_attention(LAST - 8 + j)
                if j >= 4:
                    save_x2(j - 4)
                    row_sum(j - 4)
            save_p(LAST)
            save_x2(4)
            save_attention(LAST)

            def activate(unit, m):
                e = unit % E
                n = KT * unit + m
                act.wait_ge(s.pre_done, n + 1)
                after(act, s.hid_lo_done, n - 1)
                func = (ACT.Tanh, ACT.Gelu, ACT.Silu)[e]
                act.activation(hid[:, m % 2, :], pb[m % 2][:], func, bias=b1_sb[:, e, m:m + 1]).then_inc(s.act_done, 1)
                act.wait_ge(s.act_done, n + 1)
                after(act, s.y_done, 4 * unit)
                copy(hid_hi[:, m, :], hid[:, m % 2, :]).then_inc(s.hid_hi_done, 1)

            row_sum(4)
            for m in range(KT):
                activate(0, m)
                if m < 3:
                    save_x2(5 + m)
                    row_sum(5 + m)
            act.wait_ge(s.g_sub, 1)
            act.activation(gt[:, 8:11, :], gt[:, 4:7, :], ACT.Exp).then_inc(s.g_exp, 1)
            for t in range(4):
                act.wait_ge(s.y_done, t + 1)
                copy(y_raw[:, t, :], pb[Y_BANKS[t]][:]).then_inc(s.y_saved, 1)
            for unit in range(1, 2 * E):
                for m in range(KT):
                    activate(unit, m)

        @block.vector
        def _(dve):
            link = Chain(dve, s.dve_link)

            def rest(lo, raw, hi):
                return dve.tensor_tensor(lo, raw, hi, ALU.subtract)

            def split_kv(first, end):
                for n in range(first, end):
                    dve.wait_ge(s.kv_hi_done, n + 1)
                    hi, lo = ((wk_hi, wk_lo), (wv_hi, wv_lo))[n // 8]
                    cols_ = bass.ts(n // 4 % 2, 512)
                    rest(lo[:, n % 4, cols_], kv_raw[:, n % 4, :], hi[:, n % 4, cols_]).then_inc(s.kv_lo_done, 1)

            def key_means(i):
                dve.wait_ge(s.k_raw_done, 3 * i + 3)
                dve.tensor_scalar(k_ms[:], k_ss[:], 1.0 / P, EPS, ALU.mult, ALU.add).then_inc(s.k_mean, 1)

            def norm_keys(i):
                dve.wait_ge(s.k_rsqrt, i + 1)
                for c in range(G):
                    ins = dve.scalar_tensor_tensor(out=k_raw[:, c, :], in0=k_raw[:, c, :], scalar=k_rstd[:, c:c + 1],
                                                   in1=wqk[:], op0=ALU.mult, op1=ALU.mult)
                ins.then_inc(s.k_normed, 1)

            def chunk(turn, u, first=False):
                i = 2 * turn + u
                dve.wait_ge(s.a_scores, i + 1)
                after(dve, s.a_turned, i)
                link(dve.tensor_tensor(block_p[:], pb[0][:].rearrange("p (g n) -> p g n", g=CG),
                                       blockmask[:].unsqueeze(1).to_broadcast([P, CG, P]), ALU.mult))
                dve.tensor_reduce(sc[:], block_p[:].rearrange("p g (l m) -> p g m l", m=B), AX,
                                  ALU.add).then_inc(s.a_extracted, 1)
                dve.wait_ge(s.a_extracted, i + 1)
                link(dve.tensor_reduce(sc_max[:], sc[:], AX, ALU.max))
                dve.tensor_tensor(sc_sub[:], sc[:], sc_max[:].unsqueeze(2).to_broadcast([P, CG, B]),
                                  ALU.subtract).then_inc(s.a_sub, 1)
                if not first:
                    key_means(i - 1)
                dve.wait_ge(s.a_exp, i + 1)
                link(dve.tensor_reduce(sc_sum[:], sc_exp[:], AX, ALU.add))
                link(dve.reciprocal(sc_rec[:], sc_sum[:]))
                link(dve.tensor_tensor(sc_p[:], sc_exp[:], sc_rec[:].unsqueeze(2).to_broadcast([P, CG, B]), ALU.mult))
                dve.tensor_tensor(block_p[:].rearrange("p g (l m) -> p g l m", m=B),
                                  sc_p[:].unsqueeze(2).to_broadcast([P, CG, GL, B]),
                                  blockmask[:].rearrange("p (l m) -> p l m", m=B).unsqueeze(1).to_broadcast([P, CG, GL, B]),
                                  ALU.mult).then_inc(s.a_probs, 1)
                if not first:
                    norm_keys(i - 1)
                dve.wait_ge(s.a_msg, i + 1)
                if first:
                    dve.wait_ge(s.x_dma, 16)
                xs = x1[:, :, bass.ds(i * CL, CL)]
                dve.scalar_tensor_tensor(out=xs, in0=xs, scalar=2.0, in1=pb[2][:].rearrange("p (l n) -> p n l", n=B),
                                         op0=ALU.mult, op1=ALU.add).then_inc(s.a_added, 1)

            split_kv(0, 8)
            dve.wait_ge(s.const_dma, 16 * N_CONST_DMA)
            link(dve.scalar_tensor_tensor(out=wqk[:], in0=qn_b[:], scalar=HEAD_SCALE, in1=kn_b[:],
                                          op0=ALU.mult, op1=ALU.mult))
            dve.wait_ge(s.consts, 1)
            chunk(0, 0, first=True)
            split_kv(8, 16)
            chunk(0, 1)
            with dve.Fori(1, CH // 2) as turn:
                link.turn(turn - 1, 2 * 5)
                chunk(turn, 0)
                chunk(turn, 1)
            link.leave(CH // 2 - 1)

            dve.wait_ge(s.a_added, CH)
            for half in range(2):
                bs = range(4 * half, 4 * half + 4)
                for b in bs:
                    ins = dve.bn_stats(bn[:, b, :], x1[:, b, :])
                link(ins)
                for b in bs:
                    ins = dve.bn_aggr(mv[:, b, :], bn[:, b, :])
                link(ins)
                b = slice(4 * half, 4 * half + 4)
                dve.tensor_scalar(ve[:, b], mv[:, b, 1], EPS, None, ALU.add).then_inc(s.ln_var, 1)

            def ln_stats(b):
                link(dve.bn_stats(bn[:, b, :], x1[:, b, :]))
                link(dve.bn_aggr(mv[:, b, :], bn[:, b, :]))
                dve.tensor_scalar(ve[:, b:b + 1], mv[:, b, 1:2], EPS, None, ALU.add).then_inc(s.ln_var, 1)

            def ln_apply(n, b):
                dve.wait_ge(s.ln_rstd, n)
                dve.tensor_scalar(x1[:, b, :], x1[:, b, :], mv[:, b, 0:1], rstd[:, b:b + 1],
                                  ALU.subtract, ALU.mult).then_inc(s.ln_out, 1)

            def save_lo(n, b, hi, lo, bank_):
                dve.wait_ge(s.x_hi_done, B * n + b + 1)
                cols_ = bass.ts(b, P)
                rest(lo[:, :, cols_], pb[bank_][:].rearrange("p (k t) -> p k t", k=KT), hi[:, :, cols_]).then_inc(s.x_lo_done, 1)

            for b in range(4):
                ln_apply(1, b)
            key_means(B - 1)
            for b in range(4):
                save_lo(0, b, x_hi, x_lo, b % 2)
            for b in range(4, B):
                ln_apply(2, b)
            norm_keys(B - 1)

            def sq_rest(n, parity):
                dve.wait_ge(s.q_sq_hi_done, n + 1)
                rest(q_sq_lo[:], pb[(2, 6)[parity]][:], q_sq_hi[:]).then_inc(s.q_sq_lo_done, 1)

            def mean_q(hh):
                dve.wait_ge(s.q_sums_turned, hh + 1)
                after(dve, s.q_rsqrt, hh)
                dve.tensor_scalar(q_ms[:].rearrange("p (b h) -> p b h", h=R),
                                  pb[7][:].rearrange("p (b r) -> p b r", r=P)[:, :, 0:R], 1.0 / P, EPS, ALU.mult, ALU.add).then_inc(s.q_mean, 1)

            save_lo(0, 4, x_hi, x_lo, 0)
            sq_rest(0, 0)
            for b in range(5, B):
                save_lo(0, b, x_hi, x_lo, b % 2)
            for n in range(1, 5):
                sq_rest(n, n % 2)
            mean_q(0)
            dve.wait_ge(s.gate_hi_done, 1)
            rest(gate_lo[:], gate_raw[:], gate_hi[:]).then_inc(s.gate_lo_done, 1)

            def scores(g, j):
                t, half = 8 * g + j, j // 4
                dve.wait_ge(s.s_done, t + 1)
                dve.wait_ge(s.q_rsqrt, 2 * g + 1 + half)
                for h in range(R):
                    c = R * (j % 4) + h
                    ins = dve.scalar_tensor_tensor(out=sx[:, h, :], in0=pb[0][:, bass.ts(h, P)],
                                                   scalar=q_rstd[:, half, c:c + 1], in1=mask_sb[:],
                                                   op0=ALU.mult, op1=ALU.add)
                ins.then_inc(s.s_masked, 1)
                dve.wait_ge(s.s_masked, t + 1)
                dve.tensor_reduce(neg_max[:], sx[:], AX, ALU.max, negate=True).then_inc(s.s_max, 1)

            def normalise(t):
                dve.wait_ge(s.s_exp, t + 1)
                dve.reciprocal(rsum[:], esum[:]).then_inc(s.s_rsum, 1)
                dve.wait_ge(s.s_rsum, t + 1)
                after(dve, s.p_turned, t)
                dve.tensor_tensor(pr[:], sx[:], rsum[:].unsqueeze(2).to_broadcast([P, R, P]), ALU.mult).then_inc(s.p_done, 1)

            def p_rest(t):
                dve.wait_ge(s.p_hi_done, t + 1)
                rest(pt_lo[:], pb[1][:].rearrange("p (h t) -> p h t", h=R), pt_hi[:]).then_inc(s.p_lo_done, 1)

            def add_o(t, b):
                dve.wait_ge(s.o_done, t + 1)
                dve.tensor_tensor(x1[:, b, :], x1[:, b, :], pb[4][:], ALU.add).then_inc(s.o_added, 1)

            def attention_rest(t):
                dve.wait_ge(s.at_hi_done, t + 1)
                rest(at_lo[:], pb[3][:].rearrange("p (h t) -> p h t", h=R), at_hi[:]).then_inc(s.at_lo_done, 1)

            def step(g, j, first=False, last=False):
                t = 8 * g + j
                scores(g, j)
                normalise(t)
                if j == 3 or j == 7 and not last:
                    mean_q(2 * g + 1 + j // 4)
                if not (first and j < 1):
                    p_rest(t - 1)
                if j < 3 or not last:
                    sq_rest(t + 5, (j + 1) % 2)
                if not (first and j < 2):
                    add_o(t - 2, (j - 2) % 8)
                if not (first and j < 1):
                    attention_rest(t - 1)
                if j == 1:
                    for h in range(2):
                        dve.wait_ge(s.wo_hi_done, 2 * g + h + 1)
                        rest(wo_lo[:, h, :], wo_raw[:, h, :], wo_hi[:, h, :]).then_inc(s.wo_lo_done, 1)

            for j in range(8):
                step(0, j, first=True)
            with dve.Fori(1, G - 1) as g:
                for j in range(8):
                    step(g, j)

            def x2_rest(b):
                save_lo(1, b, x2_hi, x2_lo, (2, 6)[b % 2])

            def stats_when_added(b):
                dve.wait_ge(s.o_added, LAST - B + b + 2)
                ln_stats(b)

            for j in range(3):
                step(G - 1, j, last=True)
            stats_when_added(0)
            mean_q(2 * G - 1)
            for j in range(3, 8):
                t = LAST - 7 + j
                scores(G - 1, j)
                p_rest(t - 1)
                add_o(t - 2, j - 2)
                normalise(t)
                attention_rest(t - 1)
                stats_when_added(j - 2)
                ln_apply(j, j - 3)
                if j >= 4:
                    x2_rest(j - 4)
            p_rest(LAST)
            add_o(LAST - 1, B - 2)
            stats_when_added(B - 2)
            attention_rest(LAST)
            ln_apply(8, 5)
            x2_rest(4)

            def hid_rest(unit, m):
                dve.wait_ge(s.hid_hi_done, KT * unit + m + 1)
                rest(hid_lo[:, m, :], hid[:, m % 2, :], hid_hi[:, m, :]).then_inc(s.hid_lo_done, 1)

            hid_rest(0, 0)
            add_o(LAST, B - 1)
            stats_when_added(B - 1)
            ln_apply(9, 6)
            x2_rest(5)
            hid_rest(0, 1)
            ln_apply(10, 7)
            x2_rest(6)
            hid_rest(0, 2)
            x2_rest(7)
            hid_rest(0, 3)

            v = lambda n: gt[:, n, :]
            RATIO, VS, MX, SUM, T01 = 3, 12, 13, 14, 15
            dve.wait_ge(s.means, 1)
            link(dve.tensor_scalar(v(VS), pb[2][:, B:2 * B], 1e-8, None, ALU.add))
            link(dve.reciprocal(v(MX), v(VS)))
            link(dve.tensor_tensor(v(RATIO), pb[2][:, 0:B], v(MX), ALU.mult))
            dve.wait_ge(s.logits, 1)
            for e in range(E):
                ins = dve.scalar_tensor_tensor(out=v(16 + e), in0=v(RATIO), scalar=gw_last[:, e:e + 1],
                                               in1=pb[6][:, 0:4 * B].rearrange("p (b e) -> p b e", e=4)[:, :, e],
                                               op0=ALU.mult, op1=ALU.add)
            link(ins)
            for e in range(E):
                ins = dve.tensor_scalar(v(19 + e), v(16 + e), gb_sb[:, e:e + 1], None, ALU.add)
            link(ins)
            by_batch = lambda a, z: gt[:, a:z, :].rearrange("p e b -> p b e")
            over_e = lambda n: v(n).unsqueeze(1).to_broadcast([P, E, B])
            link(dve.tensor_reduce(v(22), by_batch(19, 22), AX, ALU.max))
            dve.tensor_tensor(gt[:, 4:7, :], gt[:, 19:22, :], over_e(22), ALU.subtract).then_inc(s.g_sub, 1)
            dve.wait_ge(s.g_exp, 1)
            link(dve.tensor_reduce(v(SUM), by_batch(8, 11), AX, ALU.add))
            link(dve.reciprocal(v(T01), v(SUM)))
            link(dve.tensor_tensor(gt[:, 23:26, :], gt[:, 8:11, :], over_e(T01), ALU.mult))
            a, b_, c = v(23), v(24), v(25)
            dve.tensor_tensor(v(26), a, b_, ALU.is_ge)
            dve.tensor_tensor(v(27), a, c, ALU.is_ge)
            link(dve.tensor_tensor(v(28), b_, c, ALU.is_ge))
            dve.tensor_tensor(v(32), v(26), v(27), ALU.add)
            dve.tensor_tensor(v(33), v(26), v(28), ALU.subtract)
            link(dve.tensor_tensor(v(31), v(27), v(28), ALU.add))
            dve.tensor_scalar(v(29), v(32), -1.0, 2.0, ALU.mult, ALU.add)
            link(dve.tensor_scalar(v(30), v(33), 1.0, None, ALU.add))
            dve.tensor_scalar(onehot[:, 0], gt[:, 29:32, :], 0.0, None, ALU.is_equal)
            dve.tensor_scalar(onehot[:, 1], gt[:, 29:32, :], 1.0, None, ALU.is_equal).then_inc(s.picked, 1)
            dve.wait_ge(s.picked, 1)
            hid_rest(1, 0)
            for i in range(2):
                link(dve.tensor_tensor(gt[:, 34:37, :], onehot[:, i], gt[:, 23:26, :], ALU.mult))
                link(dve.tensor_reduce(v(37 + i), by_batch(34, 37), AX, ALU.add))
            link(dve.tensor_tensor(v(39), v(37), v(38), ALU.add))
            link(dve.tensor_scalar(v(34), v(39), 1e-8, None, ALU.add))
            link(dve.reciprocal(v(35), v(34)))
            link(dve.tensor_tensor(gt[:, 37:39, :], gt[:, 37:39, :], v(35).unsqueeze(1).to_broadcast([P, 2, B]), ALU.mult))
            dve.wait_ge(s.choice_out, 1)
            for i in range(2):
                link(dve.tensor_tensor(choice[:, i], pb[2][:, 16 + 24 * i:40 + 24 * i].rearrange("p (e b) -> p e b", e=E),
                                       v(37 + i).unsqueeze(1).to_broadcast([P, E, B]), ALU.mult))
            link(dve.tensor_tensor(coef[:], choice[:, 0], choice[:, 1], ALU.add))
            for m in range(1, KT):
                hid_rest(1, m)
            dve.wait_ge(s.b2_dma, 16 * E)

            def weigh(unit, t, src):
                b, e = 4 * (unit // E) + t, unit % E
                return dve.scalar_tensor_tensor(out=x1[:, b, :], in0=src, scalar=coef[:, e, b:b + 1],
                                                in1=x1[:, b, :], op0=ALU.mult, op1=ALU.add)

            def add_y(unit, t):
                if unit:
                    dve.wait_ge(s.y_done, 4 * unit + t + 1)
                else:
                    dve.wait_ge(s.y_saved, t + 1)
                weigh(unit, t, pb[Y_BANKS[t]][:] if unit else y_raw[:, t, :]).then_inc(s.y_added, 1)

            for unit in range(2 * E):
                if unit >= 2:
                    for m in range(KT):
                        hid_rest(unit, m)
                if unit == E:
                    for b in range(4):
                        ln_stats(b)
                    for b in range(4):
                        ln_apply(11 + b, b)
                for t in range(4):
                    ins = weigh(unit, t, b2_b[:, unit % E, :])
                link(ins)
                for t in range(4):
                    add_y(unit, t)
                    if unit == 2 * E - 1:
                        dve.wait_ge(s.y_added, 4 * unit + t + 1)
                        ln_stats(4 + t)
                        ln_apply(15 + t, 4 + t)
                dve.wait_ge(s.y_added, 4 * unit + 4)

        @block.tensor
        def _(pe):
            def three(out_ap, pairs):
                n = 3 * len(pairs)
                i = 0
                for w_hi, w_lo, m_hi, m_lo in pairs:
                    for w, m in ((w_hi, m_hi), (w_hi, m_lo), (w_lo, m_hi)):
                        ins = pe.matmul(out_ap, w, m, start=(i == 0), stop=(i == n - 1))
                        i += 1
                return ins

            def project(hi, lo, u, half, bank_):
                cols_ = bass.ts(half, 512)
                return three(pb[bank_][:], [(ctx_hi[:, u, bass.ts(k, P)], ctx_lo[:, u, bass.ts(k, P)],
                                             hi[:, k, cols_], lo[:, k, cols_]) for k in range(KT)])

            def turn_keys(i, half):
                if half == 0:
                    pe.wait_ge(s.k_normed, i + 1)
                after(pe, s.k_saved, 2 * i + half)
                for c in range(4):
                    ins = pe.transpose(pb[5][:, bass.ts(c, P)], k_raw[:, 4 * half + c, :], ident[:])
                ins.then_inc(s.k_turned, 1)

            def values(i, u, first=False):
                after(pe, s.v_saved, 2 * i)
                for half in range(2):
                    if first:
                        pe.wait_ge(s.kv_lo_done, 12 + 4 * half)
                    project(wv_hi, wv_lo, u, half, 6 + half).then_inc(s.v_done, 1)

            def chunk(turn, u, first=False):
                i = 2 * turn + u
                pe.wait_ge(s.cols_dma[u], 16 * turn + 16)
                after(pe, s.a_extracted, i)
                for c in range(CG):
                    w = cols[:, u, bass.ts(c, P)]
                    ins = pe.matmul(pb[0][:, bass.ts(c, P)], w, w, start=True, stop=True)
                ins.then_inc(s.a_scores, 1)

                def keys(half):
                    if half == 0:
                        pe.wait_ge(s.ctx_lo_done, i + 1)
                        after(pe, s.k_raw_done, 3 * i)
                    if first:
                        pe.wait_ge(s.kv_lo_done, 4 + 4 * half)
                    ins = project(wk_hi, wk_lo, u, half, 3 + half)
                    if half == 1:
                        ins.then_inc(s.projected, 1)

                def turn_probs():
                    pe.wait_ge(s.a_probs, i + 1)
                    for c in range(CG):
                        ins = pe.transpose(pb[1][:, bass.ts(c, P)], block_p[:, c, :], ident[:])
                    ins.then_inc(s.a_turned, 1)

                def messages():
                    pe.wait_ge(s.a_probs_t, i + 1)
                    pe.wait_ge(s.rows_dma[u], 16 * turn + 16)
                    after(pe, s.a_added, i)
                    for c in range(CG):
                        ins = pe.matmul(pb[2][:, bass.ts(c, P)], rows[:, u, bass.ts(c, P)], block_pt[:, c, :],
                                        start=True, stop=True)
                    ins.then_inc(s.a_msg, 1)

                if first:
                    keys(0)
                    keys(1)
                    turn_probs()
                    messages()
                else:
                    values(i - 1, (u + 1) % 2, first=isinstance(i, int))
                    turn_probs()
                    keys(0)
                    messages()
                    turn_keys(i - 1, 0)
                    keys(1)
                    turn_keys(i - 1, 1)

            pe.wait_ge(s.consts, 1)
            chunk(0, 0, first=True)
            chunk(0, 1)
            with pe.Fori(1, CH // 2) as turn:
                chunk(turn, 0)
                chunk(turn, 1)

            def turn_x(n, b, banks):
                pe.wait_ge(s.ln_out, B * n + b + 1)
                after(pe, s.x_lo_done, B * n + b - 1)
                for k in range(KT):
                    ins = pe.transpose(pb[banks[b % 2]][:, bass.ts(k, P)], x1[:, b, bass.ts(k, P)], ident[:])
                ins.then_inc(s.x_turned, 1)

            values(B - 1, 1)
            for b in range(4):
                turn_x(0, b, (0, 1))

            def query_piece(g, n, half, h, parity):
                pe.wait_ge(s.wq_lo_done, 4 * g + h + 1)
                after(pe, s.q_sq_lo_done, n - 1)
                cols_ = bass.ts(half, HALF_T)
                three(pb[(2, 6)[parity]][:], [(wq_hi[:, h, k, :], wq_lo[:, h, k, :], x_hi[:, k, cols_], x_lo[:, k, cols_])
                                              for k in range(KT)]).then_inc(s.q_done, 1)

            def query_sums(n, hh, h):
                pe.wait_ge(s.q_sq_lo_done, n + 1)
                if h == 0:
                    after(pe, s.q_row_saved, hh)
                pe.matmul(pb[5][:], head_row[:, h, :], q_sq_hi[:], start=(h == 0), stop=False)
                pe.matmul(pb[5][:], head_row[:, h, :], q_sq_lo[:], start=False, stop=(h == R - 1)).then_inc(s.q_summed, 1)

            def turn_sums(hh):
                pe.wait_ge(s.q_row_saved, hh + 1)
                after(pe, s.q_mean, hh)
                for c in range(4):
                    ins = pe.transpose(pb[7][:, bass.ts(c, P)], q_row[:, bass.ts(c, P)], ident[:])
                ins.then_inc(s.q_sums_turned, 1)

            pe.wait_ge(s.x_lo_done, 4)
            pe.wait_ge(s.v_saved, 2 * B)
            query_piece(0, 0, 0, 0, 0)
            turn_x(0, 4, (0, 1))
            turn_x(0, 5, (0, 1))
            turn_keys(B - 1, 0)
            query_piece(0, 1, 0, 1, 1)
            turn_x(0, 6, (0, 1))
            turn_x(0, 7, (0, 1))
            turn_keys(B - 1, 1)
            pe.wait_ge(s.k_saved, 2 * B)
            pe.wait_ge(s.consts, 3)
            query_sums(0, 0, 0)
            for n in range(2, 5):
                if n == 4:
                    pe.wait_ge(s.x_lo_done, B)
                query_piece(0, n, n // 4, n % 4, n % 2)
                query_sums(n - 1, 0, n - 1)
            turn_sums(0)
            query_sums(4, 1, 0)

            def scores(g, j):
                t, half = 8 * g + j, j // 4
                pe.wait_ge(s.q_saved, 8 * g + 4 + 4 * half)
                after(pe, s.s_masked, t)
                for h in range(R):
                    ins = pe.matmul(pb[0][:, bass.ts(h, P)], q_t[:, half, h, bass.ts(j % 4, P)],
                                    k_t[:, bass.ds(g, 1), bass.ts(j, P)].rearrange("p a t -> p (a t)"),
                                    start=True, stop=True)
                ins.then_inc(s.s_done, 1)

            def turn_p(t):
                pe.wait_ge(s.p_done, t + 1)
                after(pe, s.p_lo_done, t)
                for h in range(R):
                    ins = pe.transpose(pb[1][:, bass.ts(h, P)], pr[:, h, :], ident[:])
                ins.then_inc(s.p_turned, 1)

            def attend(t, g, b):
                pe.wait_ge(s.p_lo_done, t + 1)
                pe.wait_ge(s.v_lo_done, 2 * g + 1 + b // 4)
                after(pe, s.at_lo_done, t)
                flat = lambda a: a[:].rearrange("p h t -> p (h t)")
                three(pb[3][:], [(v_hi[:, b, :], v_lo[:, b, :], flat(pt_hi), flat(pt_lo))]).then_inc(s.pv_done, 1)

            def project_out(t, g):
                pe.wait_ge(s.at_lo_done, t + 1)
                pe.wait_ge(s.wo_lo_done, 2 * g + 2)
                pe.wait_ge(s.wo2_lo_done, 2 * g + 2)
                after(pe, s.o_added, t)
                three(pb[4][:], [(at_hi[:, h, :], at_lo[:, h, :], wo_hi[:, h, :], wo_lo[:, h, :])
                                 for h in range(R)]).then_inc(s.o_done, 1)

            def step(g, j, first=False, last=False):
                t = 8 * g + j
                n = t + 5
                piece = j < 3 or not last
                scores(g, j)
                if piece:
                    query_piece(g if j < 3 else g + 1, n, *PIECE[j], (j + 1) % 2)
                if j == 3 or j == 7 and not last:
                    turn_sums(2 * g + 1 + j // 4)
                if not (first and j < 1):
                    turn_p(t - 1)
                if not (first and j < 2):
                    project_out(t - 2, g if j > 1 else g - 1)
                if not (first and j < 1):
                    attend(t - 1, g if j > 0 else g - 1, (j - 1) % 8)
                if piece:
                    query_sums(n, 2 * g + (1, 1, 1, 2, 2, 2, 2, 3)[j], PIECE[j][1])

            for j in range(8):
                step(0, j, first=True)
            with pe.Fori(1, G - 1) as g:
                for j in range(8):
                    step(g, j)
            for j in range(3):
                step(G - 1, j, last=True)
            scores(G - 1, 3)
            turn_sums(2 * G - 1)
            for j in range(3, 8):
                t = LAST - 7 + j
                turn_p(t - 1)
                project_out(t - 2, G - 1)
                if j < 7:
                    scores(G - 1, j + 1)
                if j >= 4:
                    turn_x(1, j - 4, (2, 6))
                attend(t - 1, G - 1, j - 1)

            def before_activation(unit, m):
                half, e = unit // E, unit % E
                n = KT * unit + m
                pe.wait_ge(s.ff_lo_done, ff_index[0, e, KT - 1] + 1)
                pe.wait_ge(s.x_lo_done, B + 4 + 4 * half)
                after(pe, s.act_done, n - 1)
                cols_ = bass.ts(half, HALF_T)
                three(pb[m % 2][:], [(w1_hi[e][:, k, bass.ts(m, P)], w1_lo[e][:, k, bass.ts(m, P)],
                                      x2_hi[:, k, cols_], x2_lo[:, k, cols_]) for k in range(KT)]).then_inc(s.pre_done, 1)

            def output(e, m, t, finish):
                for i, (w, r) in enumerate(((hid_hi, w2_hi), (hid_hi, w2_lo), (hid_lo, w2_hi))):
                    ins = pe.matmul(pb[Y_BANKS[t]][:], w[:, m, bass.ts(t, P)], r[e][:, m, :],
                                    start=(m == 0 and i == 0), stop=(finish and i == 2))
                if finish:
                    ins.then_inc(s.y_done, 1)

            turn_p(LAST)
            project_out(LAST - 1, G - 1)
            turn_x(1, 4, (2, 6))
            attend(LAST, G - 1, B - 1)
            before_activation(0, 0)
            turn_x(1, 5, (2, 6))
            project_out(LAST, G - 1)
            before_activation(0, 1)
            turn_x(1, 6, (2, 6))
            before_activation(0, 2)
            turn_x(1, 7, (2, 6))
            before_activation(0, 3)
            pe.wait_ge(s.gate_lo_done, 1)
            pe.wait_ge(s.x_lo_done, 2 * B)
            for b in range(B):
                ins = three(pb[6][:, bass.ts(b, E + 1)],
                            [(x2_hi[:, k, bass.ts(b, P)], x2_lo[:, k, bass.ts(b, P)], gate_hi[:, k, :], gate_lo[:, k, :])
                             for k in range(KT)])
            ins.then_inc(s.logits, 1)
            pe.wait_ge(s.o_added, LAST + 1)

            for unit in range(2 * E):
                e = unit % E
                if unit:
                    for m in range(KT):
                        before_activation(unit, m)
                        if unit == 1 and m == 0:
                            pe.wait_ge(s.picked, 1)
                            pe.matmul(pb[2][:, 16:64], row0[:], onehot[:].rearrange("p i e b -> p (i e b)"),
                                      start=True, stop=True).then_inc(s.choice_out, 1)
                pe.wait_ge(s.ff_lo_done, ff_index[1, e, KT - 1] + 1)
                if unit == 1:
                    pe.wait_ge(s.y_saved, 4)
                elif unit:
                    pe.wait_ge(s.y_added, 4 * unit)
                if unit < 2 * E - 1:
                    for m in range(KT):
                        pe.wait_ge(s.hid_lo_done, KT * unit + m + 1)
                        for t in range(4):
                            output(e, m, t, m == KT - 1)
                        if unit == 0 and m == 0:
                            pe.wait_ge(s.row_sums, B)
                            pe.matmul(pb[2][:, 0:B], text_mean[:], row_abs[:], start=True, stop=True)
                            pe.matmul(pb[2][:, B:2 * B], vis_mean[:], row_abs[:], start=True,
                                      stop=True).then_inc(s.means, 1)
                else:
                    pe.wait_ge(s.hid_lo_done, KT * unit + KT)
                    for t in range(4):
                        for m in range(KT):
                            output(e, m, t, m == KT - 1)


def kernel(**inputs):
    import numpy as np
    import concourse.bacc as bacc
    from concourse.bass_utils import run_bass_kernel_spmd as run

    a = {n: np.asarray(v) for n, v in inputs.items()}
    x = a["x"]
    wk, wv = a["L0_xattn_k_proj_w"], a["L0_xattn_v_proj_w"]
    w2t = lambda w: w.reshape(2, 512, KT, P).transpose(3, 2, 0, 1)
    arrays = {
        "x_nat": x,
        "x_cols": x.transpose(1, 2, 0).reshape(P, CH, CL * B).transpose(1, 0, 2),
        "x_rows": x.transpose(2, 0, 1).reshape(CH, CG, P, P).transpose(0, 2, 1, 3).reshape(CH, P, CG * P),
        "ctx_t": a["ctx_4096"].reshape(B, P, KT, P).transpose(0, 3, 2, 1).reshape(B, P, KT * P),
        "mask": a["mask_1x1xSxS2_ff0"].reshape(P, P),
        "wq_t": a["L0_xattn_q_proj_w"].reshape(G * R, P, KT, P).transpose(0, 3, 2, 1).reshape(G * R, P, KT * P),
        "wkv_t": np.stack([w2t(w)[:, k, half] for w in (wk, wv) for half in range(2) for k in range(KT)]),
        "wo_t": a["L0_xattn_o_proj_w"].T.reshape(G, R, P, D).transpose(0, 2, 1, 3),
        "qn_w": a["L0_xattn_q_norm_w"], "kn_w": a["L0_xattn_k_norm_w"],
        "gate_wp": np.pad(a["L0_ffn_gate_w"][:D].reshape(KT, P, E).transpose(1, 0, 2), ((0, 0), (0, 0), (0, 1))),
        "gate_last": a["L0_ffn_gate_w"][D], "gate_b": a["L0_ffn_gate_b"],
        "w1": a["L0_ffn_w1"], "b1_t": a["L0_ffn_b1"].reshape(E, KT, P).transpose(2, 0, 1),
        "w2": a["L0_ffn_w2"], "b2": a["L0_ffn_b2"],
    }
    arrays = {n: np.ascontiguousarray(v) for n, v in arrays.items()}
    nc = bacc.Bacc("TRN2", target_bir_lowering=False, num_devices=1)
    aps = [nc.dram_tensor(n, v.shape, F32, kind="ExternalInput").ap() for n, v in arrays.items()]
    out = nc.dram_tensor("out", (B, P, D), F32, kind="ExternalOutput").ap()
    build(nc, *aps, out)
    r = run(nc, [arrays], core_ids=[0])
    return r.results[0]["out"]
```

```python
from contextlib import ExitStack

import concourse.bass as bass
from concourse import mybir

F32 = mybir.dt.float32
F32R = mybir.dt.float32r
ACT = mybir.ActivationFunctionType
ALU = mybir.AluOpType
AX = mybir.AxisListType.X

P = 128
B = 8
D = 512
KT = D // P
T = B * P
HALF_T = T // 2
G = 8
R = 4
CH = 8
CG = 4
GL = 16
CL = CG * GL
E = 3
VIS = int(P * 0.3)
EPS = 1e-5
PIECE = ((1, 1), (1, 2), (1, 3), (0, 0), (0, 1), (0, 2), (0, 3), (1, 0))
SELF_SCALE = float(P) ** -0.5
HEAD_SCALE = float(P) ** -0.5


class Chain:

    def __init__(self, eng, sem):
        self.eng, self.sem, self.base, self.n = eng, sem, 0, 0

    def __call__(self, ins):
        self.n += 1
        ins.then_inc(self.sem, 1)
        self.eng.wait_ge(self.sem, self.base + self.n)

    def turn(self, turns, per):
        self.ahead, self.per = self.n, per
        self.base, self.n = self.ahead + turns * per, 0

    def leave(self, turns):
        assert self.n == self.per, (self.n, self.per)
        self.base, self.n = 0, self.ahead + turns * self.per


class Semaphores:

    def __init__(self, sem):
        self.consts = sem("consts")
        self.const_dma = sem("const_dma")
        self.kv_hi_done = sem("kv_hi_done")
        self.kv_lo_done = sem("kv_lo_done")
        self.x_dma = sem("x_dma")
        self.ctx_hi_done = sem("ctx_hi_done")
        self.ctx_lo_done = sem("ctx_lo_done")
        self.a_scores = sem("a_scores")
        self.a_extracted = sem("a_extracted")
        self.a_sub = sem("a_sub")
        self.a_exp = sem("a_exp")
        self.a_probs = sem("a_probs")
        self.a_turned = sem("a_turned")
        self.a_probs_t = sem("a_probs_t")
        self.a_msg = sem("a_msg")
        self.a_added = sem("a_added")
        self.projected = sem("projected")
        self.k_raw_done = sem("k_raw_done")
        self.k_mean = sem("k_mean")
        self.k_rsqrt = sem("k_rsqrt")
        self.k_normed = sem("k_normed")
        self.k_turned = sem("k_turned")
        self.k_saved = sem("k_saved")
        self.v_done = sem("v_done")
        self.v_saved = sem("v_saved")
        self.bn_done = sem("bn_done")
        self.ln_var = sem("ln_var")
        self.ln_rstd = sem("ln_rstd")
        self.ln_out = sem("ln_out")
        self.x_turned = sem("x_turned")
        self.x_hi_done = sem("x_hi_done")
        self.x_lo_done = sem("x_lo_done")
        self.wq_hi_done = sem("wq_hi_done")
        self.wq_lo_done = sem("wq_lo_done")
        self.wo_dma = sem("wo_dma")
        self.wo_hi_done = sem("wo_hi_done")
        self.wo_lo_done = sem("wo_lo_done")
        self.wo2_hi_done = sem("wo2_hi_done")
        self.wo2_lo_done = sem("wo2_lo_done")
        self.q_done = sem("q_done")
        self.q_saved = sem("q_saved")
        self.q_squared = sem("q_squared")
        self.q_sq_hi_done = sem("q_sq_hi_done")
        self.q_sq_lo_done = sem("q_sq_lo_done")
        self.q_summed = sem("q_summed")
        self.q_row_saved = sem("q_row_saved")
        self.q_sums_turned = sem("q_sums_turned")
        self.q_mean = sem("q_mean")
        self.q_rsqrt = sem("q_rsqrt")
        self.q_first = sem("q_first")
        self.s_done = sem("s_done")
        self.s_masked = sem("s_masked")
        self.s_max = sem("s_max")
        self.s_exp = sem("s_exp")
        self.s_rsum = sem("s_rsum")
        self.p_done = sem("p_done")
        self.p_turned = sem("p_turned")
        self.p_hi_done = sem("p_hi_done")
        self.p_lo_done = sem("p_lo_done")
        self.v_hi_done = sem("v_hi_done")
        self.v_lo_done = sem("v_lo_done")
        self.pv_done = sem("pv_done")
        self.at_hi_done = sem("at_hi_done")
        self.at_lo_done = sem("at_lo_done")
        self.o_done = sem("o_done")
        self.o_added = sem("o_added")
        self.ff_hi_done = sem("ff_hi_done")
        self.ff_lo_done = sem("ff_lo_done")
        self.row_sums = sem("row_sums")
        self.means = sem("means")
        self.picked = sem("picked")
        self.choice_out = sem("choice_out")
        self.pre_done = sem("pre_done")
        self.act_done = sem("act_done")
        self.hid_hi_done = sem("hid_hi_done")
        self.hid_lo_done = sem("hid_lo_done")
        self.y_done = sem("y_done")
        self.y_saved = sem("y_saved")
        self.y_added = sem("y_added")
        self.g_sub = sem("g_sub")
        self.g_exp = sem("g_exp")
        self.gate_dma = sem("gate_dma")
        self.b2_dma = sem("b2_dma")
        self.store = sem("store")
        self.dve_link = sem("dve_link")
        self.pool_link = sem("pool_link")
        self.kv_dma = [sem(f"kv_dma{n}") for n in range(16)]
        self.ff_dma = [sem(f"ff_dma{i}") for i in range(4)]
        self.wq_dma = [sem(f"wq_dma{i}") for i in range(2)]
        self.cols_dma = [sem(f"cols_dma{i}") for i in range(2)]
        self.rows_dma = [sem(f"rows_dma{i}") for i in range(2)]
        self.ctx_dma = [sem(f"ctx_dma{i}") for i in range(2)]


def after(eng, sem, value):
    if not isinstance(value, int) or value > 0:
        eng.wait_ge(sem, value)


def build(nc, x_nat, x_cols, x_rows, ctx_t, mask, wq_t, wkv_t, wo_t, qn_w, kn_w,
          gate_wt, gate_last, gate_b, w1, b1_t, w2, b2, out):
    with ExitStack() as stack:
        cur = [(nc.sbuf_base + 63) // 64 * 64]
        at = {}

        def sb(name, shape, dt=F32):
            size = 4
            for n in shape[1:]:
                size *= n
            at[name] = cur[0]
            t = nc.alloc_sbuf_tensor_at(name, shape, dt, offset=cur[0])
            cur[0] += (size + 31) // 32 * 32
            assert cur[0] <= nc.sbuf_usable_end, (name, cur[0])
            return t

        def bank(name):
            return stack.enter_context(nc.psum_tensor(name, [P, 512], F32))

        ident = sb("ident", [P, P])
        blockmask = sb("blockmask", [P, P])
        mask_sb = sb("mask_sb", [P, P])
        text_mean = sb("text_mean", [P, P])
        vis_mean = sb("vis_mean", [P, P])
        row0 = sb("row0", [P, P])
        head_row = sb("head_row", [P, R, P], F32R)
        ones = sb("ones", [P, 1])
        neghalf = sb("neghalf", [P, 16])
        qn_b = sb("qn_b", [P, P])
        kn_b = sb("kn_b", [P, P])
        bn = sb("bn", [P, B, 6])
        mv = sb("mv", [P, B, 2])
        ve = sb("ve", [P, B])
        rstd = sb("rstd", [P, B])
        b1_sb = sb("b1_sb", [P, E, KT])
        gw_last = sb("gw_last", [P, E])
        gb_sb = sb("gb_sb", [P, E])
        q_ms = sb("q_ms", [P, 16])
        q_rstd = sb("q_rstd", [P, 2, 16])
        row_abs = sb("row_abs", [P, B])
        neg_max = sb("neg_max", [P, R])
        esum = sb("esum", [P, R])
        rsum = sb("rsum", [P, R])
        x1 = sb("x1", [P, B, D])
        wq_raw = sb("wq_raw", [P, 2, KT * P])
        wo_raw = sb("wo_raw", [P, R, D])
        ff_raw = wo_raw
        wqk = qn_b
        wq_hi = sb("wq_hi", [P, R, KT, P], F32R)
        wq_lo = sb("wq_lo", [P, R, KT, P], F32R)
        k_t = sb("k_t", [P, G, T])
        v_all = sb("v_all", [P, B, G * P])
        at_ab = cur[0]
        cur[0] = at["v_all"]
        kv_raw = sb("kv_raw", [P, 16, 512])
        assert cur[0] == at_ab
        wk_hi = sb("wk_hi", [P, KT, G * P], F32R)
        wk_lo = sb("wk_lo", [P, KT, G * P], F32R)
        wv_hi = sb("wv_hi", [P, KT, G * P], F32R)
        wv_lo = sb("wv_lo", [P, KT, G * P], F32R)
        cols = sb("cols", [P, 2, 512])
        rows = sb("rows", [P, 2, 512])
        ctx_raw = sb("ctx_raw", [P, 2, 512])
        ctx_hi = sb("ctx_hi", [P, 2, 512], F32R)
        ctx_lo = sb("ctx_lo", [P, 2, 512], F32R)
        block_p = sb("block_p", [P, CG, P])
        block_pt = sb("block_pt", [P, CG, P])
        sc = sb("sc", [P, CG, B])
        sc_max = sb("sc_max", [P, CG])
        sc_sub = sb("sc_sub", [P, CG, B])
        sc_exp = sb("sc_exp", [P, CG, B])
        sc_sum = sb("sc_sum", [P, CG])
        sc_rec = sb("sc_rec", [P, CG])
        sc_p = sb("sc_p", [P, CG, B])
        k_raw = sb("k_raw", [P, G, P])
        k_ss = sb("k_ss", [P, G])
        k_ms = sb("k_ms", [P, G])
        k_rstd = sb("k_rstd", [P, G])
        cur[0] = at_ab
        x_hi = sb("x_hi", [P, KT, T], F32R)
        x_lo = sb("x_lo", [P, KT, T], F32R)
        q_t = sb("q_t", [P, 2, R, HALF_T])
        wo_hi = sb("wo_hi", [P, R, D], F32R)
        wo_lo = sb("wo_lo", [P, R, D], F32R)
        sx = sb("sx", [P, R, P])
        pr = sb("pr", [P, R, P])
        at_rest = cur[0]
        q_sq_hi = sb("q_sq_hi", [P, HALF_T], F32R)
        q_sq_lo = sb("q_sq_lo", [P, HALF_T], F32R)
        q_row = sb("q_row", [P, HALF_T])
        v_hi = sb("v_hi", [P, B, P], F32R)
        v_lo = sb("v_lo", [P, B, P], F32R)
        pt_hi = sb("pt_hi", [P, R, P], F32R)
        pt_lo = sb("pt_lo", [P, R, P], F32R)
        at_hi = sb("at_hi", [P, R, P], F32R)
        at_lo = sb("at_lo", [P, R, P], F32R)
        w1_hi, w1_lo, w2_hi, w2_lo = [None] * E, [None] * E, [None] * E, [None] * E

        def place(where, e, hi, lo, name):
            cur[0] = where
            hi[e] = sb(f"{name}_hi{e}", [P, KT, D], F32R)
            lo[e] = sb(f"{name}_lo{e}", [P, KT, D], F32R)
            return cur[0]

        place(place(at["x_hi"], 0, w1_hi, w1_lo, "w1"), 0, w2_hi, w2_lo, "w2")
        place(at["wq_hi"], 1, w1_hi, w1_lo, "w1")
        place(place(at["k_t"], 1, w2_hi, w2_lo, "w2"), 2, w1_hi, w1_lo, "w1")
        place(at["wo_hi"], 2, w2_hi, w2_lo, "w2")
        cur[0] = at["v_all"]
        x2_hi = sb("x2_hi", [P, KT, T], F32R)
        x2_lo = sb("x2_lo", [P, KT, T], F32R)
        cur[0] = at["q_t"]
        hid_hi = sb("hid_hi", [P, KT, HALF_T], F32R)
        hid_lo = sb("hid_lo", [P, KT, HALF_T], F32R)
        cur[0] = at["sx"]
        hid = sb("hid", [P, 2, HALF_T])
        cur[0] = at_rest
        junk = sb("junk", [P, D])
        gate_2 = sb("gate_2", [P, D])
        junk_b = sb("junk_b", [P, D])
        b2_b = sb("b2_b", [P, E, D])
        y_raw = sb("y_raw", [P, 4, D])
        gt = sb("gt", [P, 40, B])
        onehot = sb("onehot", [P, 2, E, B])
        choice = sb("choice", [P, 2, E, B])
        coef = sb("coef", [P, E, B])

        gate_e = (wq_raw[:, 0, :], wq_raw[:, 1, :], gate_2[:])

        pb = [bank(f"bank{i}") for i in range(8)]
        X_BANKS = (0, 1, 3, 4)
        Y_BANKS = (3, 4, 5, 7)
        s = Semaphores(lambda name: stack.enter_context(nc.semaphore(name)))
        N_CONST_DMA = 6
        block = stack.enter_context(nc.Block())

        FF = [(w, e, k) for e in range(E) for w in (0, 1) for k in range(KT)]
        ff_index = {wek: n for n, wek in enumerate(FF)}
        LAST = G * B - 1

        @block.sync
        def _(sp):
            flat = lambda a: a.rearrange("a p n -> p (a n)")

            def load_kv(n):
                sp.dma_start(kv_raw[:, n, :], wkv_t[n]).then_inc(s.kv_dma[n], 16)

            sp.dma_start(cols[:, 0, :], x_cols[0]).then_inc(s.cols_dma[0], 16)
            sp.dma_start(ctx_raw[:, 0, :], ctx_t[0]).then_inc(s.ctx_dma[0], 16)
            for n in range(8):
                load_kv(n)
            one = lambda a: a.rearrange("(a d) -> a d", a=1)
            for dst, src in (
                (qn_b[:], one(qn_w).to_broadcast([P, P])), (kn_b[:], one(kn_w).to_broadcast([P, P])),
                (mask_sb[:], mask), (b1_sb[:], b1_t),
                (gw_last[:], one(gate_last).to_broadcast([P, E])), (gb_sb[:], one(gate_b).to_broadcast([P, E])),
            ):
                sp.dma_start(dst, src).then_inc(s.const_dma, 16)
            sp.dma_start(rows[:, 0, :], x_rows[0]).then_inc(s.rows_dma[0], 16)
            for n in range(8, 12):
                load_kv(n)
            sp.dma_start(cols[:, 1, :], x_cols[1]).then_inc(s.cols_dma[1], 16)
            sp.dma_start(ctx_raw[:, 1, :], ctx_t[1]).then_inc(s.ctx_dma[1], 16)
            for n in range(12, 16):
                load_kv(n)
            sp.dma_start(x1[:], x_nat.rearrange("b c l -> c b l")).then_inc(s.x_dma, 16)
            sp.dma_start(rows[:, 1, :], x_rows[1]).then_inc(s.rows_dma[1], 16)
            for m in range(2):
                sp.dma_start(wq_raw[:, m, :], wq_t[m]).then_inc(s.wq_dma[m], 16)
            with sp.Fori(1, CH // 2) as turn:
                for u in range(2):
                    i = 2 * turn + u
                    sp.wait_ge(s.ctx_lo_done, i - 1)
                    sp.dma_start(ctx_raw[:, u, :], flat(ctx_t[bass.ds(i, 1)])).then_inc(s.ctx_dma[u], 16)
                    sp.wait_ge(s.a_scores, i - 1)
                    sp.dma_start(cols[:, u, :], flat(x_cols[bass.ds(i, 1)])).then_inc(s.cols_dma[u], 16)
                    sp.wait_ge(s.a_msg, i - 1)
                    sp.dma_start(rows[:, u, :], flat(x_rows[bass.ds(i, 1)])).then_inc(s.rows_dma[u], 16)
            sp.dma_start(wo_raw[:], wo_t[0]).then_inc(s.wo_dma, 16)
            for m in range(2, 4):
                sp.wait_ge(s.wq_lo_done, m - 1)
                sp.dma_start(wq_raw[:, m % 2, :], wq_t[m]).then_inc(s.wq_dma[m % 2], 16)
            with sp.Fori(0, G - 1) as g:
                for h in range(R):
                    m = 4 * g + 4 + h
                    sp.wait_ge(s.wq_lo_done, m - 1)
                    sp.dma_start(wq_raw[:, h % 2, :], flat(wq_t[bass.ds(m, 1)])).then_inc(s.wq_dma[h % 2], 16)
                    if h == 1:
                        sp.wait_ge(s.wo_lo_done, 2 * g + 2)
                        sp.wait_ge(s.wo2_lo_done, 2 * g + 2)
                        sp.dma_start(wo_raw[:], wo_t[bass.ds(g + 1, 1)].rearrange("a p h n -> p (a h) n")).then_inc(s.wo_dma, 16)
            sp.wait_ge(s.wo_lo_done, 2 * G)
            sp.wait_ge(s.wo2_lo_done, 2 * G)

            def load_ff(first, end):
                for n in range(first, end):
                    w, e, k = FF[n]
                    after(sp, s.ff_lo_done, n - 3)
                    sp.dma_start(ff_raw[:, n % 4, :], (w1, w2)[w][e, k * P:(k + 1) * P, :]).then_inc(s.ff_dma[n % 4], 16)

            load_ff(0, 4)
            sp.wait_ge(s.wq_lo_done, G * R)
            sp.wait_ge(s.q_summed, G * B)
            for e in range(E):
                sp.dma_start(gate_e[e], gate_wt[e:e + 1, :].to_broadcast([P, D])).then_inc(s.gate_dma, 16)
            load_ff(4, 24)
            sp.wait_ge(s.at_lo_done, LAST + 1)
            sp.wait_ge(s.o_done, LAST + 1)
            for e in range(E):
                sp.dma_start(b2_b[:, e, :], b2[e:e + 1, :].to_broadcast([P, D])).then_inc(s.b2_dma, 16)
            for b in range(B):
                sp.wait_ge(s.ln_out, 2 * B + b + 1)
                sp.dma_start(out[b], x1[:, b, :]).then_inc(s.store, 16)
            sp.wait_ge(s.store, 16 * B)

        @block.gpsimd
        def _(pool):
            link = Chain(pool, s.pool_link)

            def keep(t, compare, base, pattern, per_partition):
                link(pool.affine_select(out=t, in_=t, compare_op=compare, fill=0.0, base=base,
                                        pattern=pattern, channel_multiplier=per_partition))

            link(pool.memset(ident[:], 1.0))
            keep(ident[:], ALU.is_equal, 0, [[-1, P]], 1)
            bm = blockmask[:].rearrange("p (l m) -> p l m", m=B)
            link(pool.memset(blockmask[:], 1.0))
            keep(bm, ALU.is_ge, 0, [[-B, GL], [0, B]], 1)
            keep(bm, ALU.is_ge, B - 1, [[B, GL], [0, B]], -1)
            pool.memset(ones[:], 1.0)
            pool.memset(neghalf[:], -0.5).then_inc(s.consts, 1)
            pool.wait_ge(s.consts, 1)

            def rsqrt(dst, src, n):
                return pool.tensor_tensor(dst, src, neghalf[:, 0:n], ALU.pow)

            def split(hi, lo, raw, hi_done, lo_done, n):
                shape = list(raw.shape)
                unit = ones[:] if len(shape) == 2 else ones[:].unsqueeze(1)
                pool.tensor_tensor(hi, raw, unit.to_broadcast(shape), ALU.mult).then_inc(hi_done, 1)
                pool.wait_ge(hi_done, n + 1)
                pool.tensor_tensor(lo, raw, hi, ALU.subtract).then_inc(lo_done, 1)

            def split_ctx(turn, u):
                c = 2 * turn + u
                pool.wait_ge(s.ctx_dma[u], 16 * turn + 16)
                after(pool, s.v_done, 2 * (c - 1))
                split(ctx_hi[:, u, :], ctx_lo[:, u, :], ctx_raw[:, u, :], s.ctx_hi_done, s.ctx_lo_done, c)

            split_ctx(0, 0)
            pool.wait_ge(s.ctx_dma[1], 16)
            split(ctx_hi[:, 1, :], ctx_lo[:, 1, :], ctx_raw[:, 1, :], s.ctx_hi_done, s.ctx_lo_done, 1)
            pool.affine_select(out=head_row[:], in_=ones[:].unsqueeze(1).to_broadcast([P, R, P]), compare_op=ALU.is_equal,
                               fill=0.0, base=0, pattern=[[1, R], [-1, P]], channel_multiplier=0).then_inc(s.consts, 1)
            link(pool.memset(text_mean[:], 1.0 / ((P - VIS) * D)))
            keep(text_mean[:], ALU.is_ge, -VIS, [[0, P]], 1)
            link(pool.memset(vis_mean[:], 1.0 / (VIS * D)))
            keep(vis_mean[:], ALU.is_ge, VIS - 1, [[0, P]], -1)
            link(pool.memset(row0[:], 1.0))
            pool.affine_select(out=row0[:], in_=row0[:], compare_op=ALU.is_ge, fill=0.0, base=0,
                               pattern=[[0, P]], channel_multiplier=-1).then_inc(s.consts, 1)

            def keys_rsqrt(i):
                pool.wait_ge(s.k_mean, i + 1)
                rsqrt(k_rstd[:], k_ms[:], G).then_inc(s.k_rsqrt, 1)

            with pool.Fori(0, CH // 2 - 1) as turn:
                for u in range(2):
                    keys_rsqrt(2 * turn + u)
                    split_ctx(turn + 1, u)
            keys_rsqrt(B - 2)

            def split_wq(g, h, with_v=None):
                raw = wq_raw[:, h % 2, :].rearrange("p (k d) -> p k d", k=KT)
                unit = ones[:].unsqueeze(1)
                pool.wait_ge(s.wq_dma[h % 2], 32 * g + 16 * (h // 2 + 1))
                pool.tensor_tensor(wq_hi[:, h], raw, unit.to_broadcast([P, KT, P]), ALU.mult).then_inc(s.wq_hi_done, 1)
                if with_v:
                    vg, half = with_v
                    b = slice(4 * half, 4 * half + 4)
                    v_raw = v_all[:, b, bass.ds(vg * P, P)]
                    pool.tensor_tensor(v_hi[:, b, :], v_raw, unit.to_broadcast([P, 4, P]), ALU.mult).then_inc(s.v_hi_done, 1)
                    pool.wait_ge(s.v_hi_done, 2 * vg + half + 1)
                pool.wait_ge(s.wq_hi_done, 4 * g + h + 1)
                pool.tensor_tensor(wq_lo[:, h], raw, wq_hi[:, h], ALU.subtract).then_inc(s.wq_lo_done, 1)
                if with_v:
                    pool.tensor_tensor(v_lo[:, b, :], v_raw, v_hi[:, b, :], ALU.subtract).then_inc(s.v_lo_done, 1)

            for h in range(3):
                split_wq(0, h)
            for half in range(2):
                pool.wait_ge(s.ln_var, half + 1)
                b = slice(4 * half, 4 * half + 4)
                rsqrt(rstd[:, b], ve[:, b], 4).then_inc(s.ln_rstd, 1)
            keys_rsqrt(B - 1)
            split_wq(0, 3)

            def split_v(g, half):
                b = slice(4 * half, 4 * half + 4)
                split(v_hi[:, b, :], v_lo[:, b, :], v_all[:, b, bass.ds(g * P, P)], s.v_hi_done, s.v_lo_done, 2 * g + half)

            def half_rsqrt(hh, half):
                pool.wait_ge(s.q_mean, hh + 1)
                rsqrt(q_rstd[:, half, :], q_ms[:], 16).then_inc(s.q_rsqrt, 1)

            def split_wo(g):
                pool.wait_ge(s.wo_dma, 16 * g + 16)
                after(pool, s.o_done, 8 * g)
                for h in (2, 3):
                    split(wo_hi[:, h, :], wo_lo[:, h, :], wo_raw[:, h, :], s.wo2_hi_done, s.wo2_lo_done, 2 * g + h - 2)

            pool.wait_ge(s.v_saved, 2 * B)
            pool.wait_ge(s.k_saved, 2 * B)
            split_v(0, 0)
            split_wo(0)
            pool.wait_ge(s.q_mean, 1)
            rsqrt(q_rstd[:, 0, 0:R], q_ms[:, 0:R], R).then_inc(s.q_first, 1)
            rsqrt(q_rstd[:, 0, R:16], q_ms[:, R:16], 16 - R).then_inc(s.q_rsqrt, 1)

            def step(g, j, first=False, last=False):
                if j == 0 and not last:
                    pool.wait_ge(s.q_done, 8 * g + 5)
                    split_wq(g + 1, 0)
                if j == 1 and not first:
                    split_wo(g)
                if j == 2:
                    after(pool, s.pv_done, 8 * g)
                    if last:
                        split_v(g, 1)
                    else:
                        pool.wait_ge(s.q_done, 8 * g + 6)
                        split_wq(g + 1, 1, with_v=(g, 1))
                if j == 3:
                    half_rsqrt(2 * g + 1, 1)
                if j == 4 and not last:
                    pool.wait_ge(s.q_done, 8 * g + 7)
                    split_wq(g + 1, 2)
                if j == 5 and not last:
                    pool.wait_ge(s.pv_done, 8 * g + 4)
                    pool.wait_ge(s.q_done, 8 * g + 8)
                    split_wq(g + 1, 3, with_v=(g + 1, 0))
                if j == 7 and not last:
                    half_rsqrt(2 * g + 2, 0)

            for j in range(8):
                step(0, j, first=True)
            with pool.Fori(1, G - 1) as g:
                for j in range(8):
                    step(g, j)
            for j in range(4):
                step(G - 1, j, last=True)

            def ln_rsqrt(n, b):
                pool.wait_ge(s.ln_var, n)
                rsqrt(rstd[:, b:b + 1], ve[:, b:b + 1], 1).then_inc(s.ln_rstd, 1)

            def split_ff(first, end):
                for n in range(first, end):
                    w, e, k = FF[n]
                    hi, lo = ((w1_hi, w1_lo), (w2_hi, w2_lo))[w]
                    pool.wait_ge(s.ff_dma[n % 4], 16 * (n // 4 + 1))
                    split(hi[e][:, k, :], lo[e][:, k, :], ff_raw[:, n % 4, :], s.ff_hi_done, s.ff_lo_done, n)

            pool.wait_ge(s.q_done, 8 * G)
            for b in range(6):
                split_ff(2 * b, 2 * b + 2)
                ln_rsqrt(3 + b, b)
            pool.wait_ge(s.s_done, LAST + 1)
            ln_rsqrt(9, 6)
            split_ff(12, 13)
            ln_rsqrt(10, 7)
            split_ff(13, 20)
            pool.wait_ge(s.o_done, LAST + 1)
            split_ff(20, 24)
            for b in range(B):
                ln_rsqrt(11 + b, b)

        @block.scalar
        def _(act):
            def copy(dst, src):
                return act.activation(dst, src, ACT.Copy)

            def split_kv(first, end):
                for n in range(first, end):
                    act.wait_ge(s.kv_dma[n], 16)
                    hi = (wk_hi, wv_hi)[n // 8]
                    copy(hi[:, n % 4, bass.ts(n // 4 % 2, 512)], kv_raw[:, n, :]).then_inc(s.kv_hi_done, 1)

            def save_keys(i, half):
                act.wait_ge(s.k_turned, 2 * i + half + 1)
                copy(k_t[:, 4 * half:4 * half + 4, bass.ds(i * P, P)], pb[5][:]).then_inc(s.k_saved, 1)

            def save_values(i, half):
                act.wait_ge(s.v_done, 2 * i + half + 1)
                dst = v_all[:, bass.ds(i, 1), bass.ts(half, 512)].rearrange("p a n -> p (a n)")
                copy(dst, pb[6 + half][:]).then_inc(s.v_saved, 1)

            def chunk(turn, u, first=False):
                i = 2 * turn + u
                act.wait_ge(s.a_sub, i + 1)
                act.activation(sc_exp[:], sc_sub[:], ACT.Exp, scale=SELF_SCALE).then_inc(s.a_exp, 1)
                if first:
                    split_kv(4, 12)
                else:
                    for half in range(2):
                        save_values(i - 1, half)
                act.wait_ge(s.a_turned, i + 1)
                after(act, s.a_msg, i)
                copy(block_pt[:], pb[1][:]).then_inc(s.a_probs_t, 1)
                if not first:
                    for half in range(2):
                        save_keys(i - 1, half)
                act.wait_ge(s.projected, i + 1)
                for half in range(2):
                    copy(k_raw[:, 4 * half:4 * half + 4, :], pb[3 + half][:]).then_inc(s.k_raw_done, 1)
                if first:
                    split_kv(12, 16)
                act.wait_ge(s.k_raw_done, 3 * i + 2)
                for half in range(2):
                    for c in range(4):
                        bank_ = pb[3 + half][:, bass.ts(c, P)]
                        ins = act.activation(bank_, bank_, ACT.Square, accum_out=k_ss[:, 4 * half + c:4 * half + c + 1])
                ins.then_inc(s.k_raw_done, 1)

            split_kv(0, 4)
            chunk(0, 0, first=True)
            chunk(0, 1)
            with act.Fori(1, CH // 2) as turn:
                chunk(turn, 0)
                chunk(turn, 1)

            def save_hi(n, b, hi, bank_):
                act.wait_ge(s.x_turned, B * n + b + 1)
                copy(hi[:, :, bass.ts(b, P)], pb[bank_][:].rearrange("p (k t) -> p k t", k=KT)).then_inc(s.x_hi_done, 1)

            save_values(B - 1, 0)
            for b in range(4):
                save_hi(0, b, x_hi, X_BANKS[b])
            save_values(B - 1, 1)

            def save_q(n, half, h, parity):
                act.wait_ge(s.q_done, n + 1)
                copy(q_t[:, half, h, :], pb[(2, 6)[parity]][:]).then_inc(s.q_saved, 1)

            def square_q(n, parity):
                bank_ = pb[(2, 6)[parity]][:]
                act.wait_ge(s.q_saved, n + 1)
                act.activation(bank_, bank_, ACT.Square).then_inc(s.q_squared, 1)
                act.wait_ge(s.q_squared, n + 1)
                after(act, s.q_summed, n)
                copy(q_sq_hi[:], bank_).then_inc(s.q_sq_hi_done, 1)

            def save_sums(hh):
                act.wait_ge(s.q_summed, 4 * hh + 4)
                after(act, s.q_sums_turned, hh)
                copy(q_row[:], pb[5][:]).then_inc(s.q_row_saved, 1)

            save_q(0, 0, 0, 0)
            save_hi(0, 4, x_hi, X_BANKS[0])
            square_q(0, 0)
            save_hi(0, 5, x_hi, X_BANKS[1])
            save_keys(B - 1, 0)
            save_q(1, 0, 1, 1)
            save_keys(B - 1, 1)
            save_hi(0, 6, x_hi, X_BANKS[2])
            save_hi(0, 7, x_hi, X_BANKS[3])
            square_q(1, 1)

            def wo_hi_parts(g):
                act.wait_ge(s.wo_dma, 16 * g + 16)
                after(act, s.o_done, 8 * g)
                for h in range(2):
                    copy(wo_hi[:, h, :], wo_raw[:, h, :]).then_inc(s.wo_hi_done, 1)

            for n in range(2, 5):
                save_q(n, n // 4, n % 4, n % 2)
                if n == 4:
                    save_sums(0)
                square_q(n, n % 2)
            wo_hi_parts(0)
            def exps(t):
                act.wait_ge(s.s_max, t + 1)
                for h in range(R):
                    ins = act.activation(sx[:, h, :], sx[:, h, :], ACT.Exp, bias=neg_max[:, h:h + 1],
                                         accum_out=esum[:, h:h + 1])
                ins.then_inc(s.s_exp, 1)

            def save_p(t):
                act.wait_ge(s.p_turned, t + 1)
                after(act, s.pv_done, t)
                copy(pt_hi[:], pb[1][:]).then_inc(s.p_hi_done, 1)

            def save_attention(t):
                act.wait_ge(s.pv_done, t + 1)
                after(act, s.o_done, t)
                copy(at_hi[:], pb[3][:]).then_inc(s.at_hi_done, 1)

            def step(g, j, first=False, last=False):
                t = 8 * g + j
                n = t + 5
                piece = j < 3 or not last
                if j == 3 or j == 7:
                    save_sums(2 * g + 1 + j // 4)
                if first and j == 0:
                    save_q(n, *PIECE[j], (j + 1) % 2)
                    square_q(n, (j + 1) % 2)
                if first and j == 1:
                    save_p(t - 1)
                exps(t)
                if piece and not (first and j == 0):
                    save_q(n, *PIECE[j], (j + 1) % 2)
                if not (first and j < 2):
                    save_p(t - 1)
                if piece and not (first and j == 0):
                    square_q(n, (j + 1) % 2)
                if not (first and j < 1):
                    save_attention(t - 1)
                if j == 1 and not first:
                    wo_hi_parts(g)

            for j in range(8):
                step(0, j, first=True)
            with act.Fori(1, G - 1) as g:
                for j in range(8):
                    step(g, j)
            for j in range(3):
                step(G - 1, j, last=True)

            def row_sum(b):
                act.wait_ge(s.ln_out, B + b + 1)
                after(act, s.row_sums, b)
                act.activation(junk[:], x1[:, b, :], ACT.Abs, accum_out=row_abs[:, b:b + 1]).then_inc(s.row_sums, 1)

            def save_x2(b):
                save_hi(1, b, x2_hi, (2, 6)[b % 2])

            save_sums(2 * G - 1)
            act.wait_ge(s.q_summed, 8 * G)
            act.wait_ge(s.v_lo_done, 2 * G)
            for j in range(3, 8):
                save_p(LAST - 8 + j)
                exps(LAST - 7 + j)
                save_attention(LAST - 8 + j)
                if j >= 4:
                    save_x2(j - 4)
                    row_sum(j - 4)
            save_p(LAST)
            save_x2(4)
            save_attention(LAST)

            def activate(unit, m):
                e = unit % E
                n = KT * unit + m
                act.wait_ge(s.pre_done, n + 1)
                after(act, s.hid_lo_done, n - 1)
                func = (ACT.Tanh, ACT.Gelu, ACT.Silu)[e]
                act.activation(hid[:, m % 2, :], pb[m % 2][:], func, bias=b1_sb[:, e, m:m + 1]).then_inc(s.act_done, 1)
                act.wait_ge(s.act_done, n + 1)
                after(act, s.y_done, 4 * unit)
                copy(hid_hi[:, m, :], hid[:, m % 2, :]).then_inc(s.hid_hi_done, 1)

            row_sum(4)
            for m in range(KT):
                activate(0, m)
                if m < 3:
                    save_x2(5 + m)
                    row_sum(5 + m)
            for t in range(4):
                act.wait_ge(s.y_done, t + 1)
                copy(y_raw[:, t, :], pb[Y_BANKS[t]][:]).then_inc(s.y_saved, 1)
            for m in range(KT):
                activate(1, m)
            act.wait_ge(s.g_sub, 1)
            act.activation(gt[:, 8:11, :], gt[:, 4:7, :], ACT.Exp).then_inc(s.g_exp, 1)
            for unit in range(2, 2 * E):
                for m in range(KT):
                    activate(unit, m)

        @block.vector
        def _(dve):
            link = Chain(dve, s.dve_link)

            def rest(lo, raw, hi):
                return dve.tensor_tensor(lo, raw, hi, ALU.subtract)

            def split_kv(first, end):
                for n in range(first, end):
                    dve.wait_ge(s.kv_hi_done, n + 1)
                    hi, lo = ((wk_hi, wk_lo), (wv_hi, wv_lo))[n // 8]
                    cols_ = bass.ts(n // 4 % 2, 512)
                    rest(lo[:, n % 4, cols_], kv_raw[:, n, :], hi[:, n % 4, cols_]).then_inc(s.kv_lo_done, 1)

            def key_means(i):
                dve.wait_ge(s.k_raw_done, 3 * i + 3)
                dve.tensor_scalar(k_ms[:], k_ss[:], 1.0 / P, EPS, ALU.mult, ALU.add).then_inc(s.k_mean, 1)

            def norm_keys(i):
                dve.wait_ge(s.k_rsqrt, i + 1)
                for c in range(G):
                    ins = dve.scalar_tensor_tensor(out=k_raw[:, c, :], in0=k_raw[:, c, :], scalar=k_rstd[:, c:c + 1],
                                                   in1=wqk[:], op0=ALU.mult, op1=ALU.mult)
                ins.then_inc(s.k_normed, 1)

            def chunk(turn, u, first=False):
                i = 2 * turn + u
                dve.wait_ge(s.a_scores, i + 1)
                after(dve, s.a_turned, i)
                link(dve.tensor_tensor(block_p[:], pb[0][:].rearrange("p (g n) -> p g n", g=CG),
                                       blockmask[:].unsqueeze(1).to_broadcast([P, CG, P]), ALU.mult))
                dve.tensor_reduce(sc[:], block_p[:].rearrange("p g (l m) -> p g m l", m=B), AX,
                                  ALU.add).then_inc(s.a_extracted, 1)
                dve.wait_ge(s.a_extracted, i + 1)
                link(dve.tensor_reduce(sc_max[:], sc[:], AX, ALU.max))
                dve.tensor_tensor(sc_sub[:], sc[:], sc_max[:].unsqueeze(2).to_broadcast([P, CG, B]),
                                  ALU.subtract).then_inc(s.a_sub, 1)
                if first:
                    split_kv(0, 4)
                else:
                    key_means(i - 1)
                dve.wait_ge(s.a_exp, i + 1)
                link(dve.tensor_reduce(sc_sum[:], sc_exp[:], AX, ALU.add))
                link(dve.reciprocal(sc_rec[:], sc_sum[:]))
                link(dve.tensor_tensor(sc_p[:], sc_exp[:], sc_rec[:].unsqueeze(2).to_broadcast([P, CG, B]), ALU.mult))
                dve.tensor_tensor(block_p[:].rearrange("p g (l m) -> p g l m", m=B),
                                  sc_p[:].unsqueeze(2).to_broadcast([P, CG, GL, B]),
                                  blockmask[:].rearrange("p (l m) -> p l m", m=B).unsqueeze(1).to_broadcast([P, CG, GL, B]),
                                  ALU.mult).then_inc(s.a_probs, 1)
                if first:
                    split_kv(4, 8)
                else:
                    norm_keys(i - 1)
                    if isinstance(i, int):
                        dve.wait_ge(s.x_dma, 16)
                        add_messages(0)
                    add_messages(i)

            def add_messages(i):
                dve.wait_ge(s.a_msg, i + 1)
                xs = x1[:, :, bass.ds(i * CL, CL)]
                dve.scalar_tensor_tensor(out=xs, in0=xs, scalar=2.0, in1=pb[2][:].rearrange("p (l n) -> p n l", n=B),
                                         op0=ALU.mult, op1=ALU.add).then_inc(s.a_added, 1)

            dve.wait_ge(s.consts, 1)
            chunk(0, 0, first=True)
            dve.wait_ge(s.const_dma, 16 * N_CONST_DMA)
            link(dve.scalar_tensor_tensor(out=wqk[:], in0=qn_b[:], scalar=HEAD_SCALE, in1=kn_b[:],
                                          op0=ALU.mult, op1=ALU.mult))
            split_kv(8, 16)
            chunk(0, 1)
            with dve.Fori(1, CH // 2) as turn:
                link.turn(turn - 1, 2 * 5)
                chunk(turn, 0)
                chunk(turn, 1)
            link.leave(CH // 2 - 1)

            dve.wait_ge(s.a_added, CH)
            def ln_first(half):
                for b in range(4 * half, 4 * half + 4):
                    ins = dve.bn_aggr(mv[:, b, :], bn[:, b, :])
                link(ins)
                b = slice(4 * half, 4 * half + 4)
                dve.tensor_scalar(ve[:, b], mv[:, b, 1], EPS, None, ALU.add).then_inc(s.ln_var, 1)

            for b in range(4):
                ins = dve.bn_stats(bn[:, b, :], x1[:, b, :])
            link(ins)
            ln_first(0)
            for b in range(4, 6):
                dve.bn_stats(bn[:, b, :], x1[:, b, :])

            def ln_stats(b):
                link(dve.bn_stats(bn[:, b, :], x1[:, b, :]))
                link(dve.bn_aggr(mv[:, b, :], bn[:, b, :]))
                dve.tensor_scalar(ve[:, b:b + 1], mv[:, b, 1:2], EPS, None, ALU.add).then_inc(s.ln_var, 1)

            def ln_apply(n, b):
                dve.wait_ge(s.ln_rstd, n)
                dve.tensor_scalar(x1[:, b, :], x1[:, b, :], mv[:, b, 0:1], rstd[:, b:b + 1],
                                  ALU.subtract, ALU.mult).then_inc(s.ln_out, 1)

            def save_lo(n, b, hi, lo, bank_):
                dve.wait_ge(s.x_hi_done, B * n + b + 1)
                cols_ = bass.ts(b, P)
                rest(lo[:, :, cols_], pb[bank_][:].rearrange("p (k t) -> p k t", k=KT), hi[:, :, cols_]).then_inc(s.x_lo_done, 1)

            for b in range(4):
                ln_apply(1, b)
            for b in range(6, B):
                ins = dve.bn_stats(bn[:, b, :], x1[:, b, :])
            link(ins)
            ln_first(1)
            key_means(B - 1)
            for b in range(4):
                save_lo(0, b, x_hi, x_lo, X_BANKS[b % 4])
            for b in range(4, B):
                ln_apply(2, b)
            norm_keys(B - 1)

            def sq_rest(n, parity):
                dve.wait_ge(s.q_sq_hi_done, n + 1)
                rest(q_sq_lo[:], pb[(2, 6)[parity]][:], q_sq_hi[:]).then_inc(s.q_sq_lo_done, 1)

            def mean_q(hh):
                dve.wait_ge(s.q_sums_turned, hh + 1)
                after(dve, s.q_rsqrt, hh)
                dve.tensor_scalar(q_ms[:].rearrange("p (b h) -> p b h", h=R),
                                  pb[7][:].rearrange("p (b r) -> p b r", r=P)[:, :, 0:R], 1.0 / P, EPS, ALU.mult, ALU.add).then_inc(s.q_mean, 1)

            save_lo(0, 4, x_hi, x_lo, X_BANKS[0])
            sq_rest(0, 0)
            for b in range(5, B):
                save_lo(0, b, x_hi, x_lo, X_BANKS[b % 4])

            def wo_rest(g):
                for h in range(2):
                    dve.wait_ge(s.wo_hi_done, 2 * g + h + 1)
                    rest(wo_lo[:, h, :], wo_raw[:, h, :], wo_hi[:, h, :]).then_inc(s.wo_lo_done, 1)

            for n in range(1, 5):
                sq_rest(n, n % 2)
            mean_q(0)
            wo_rest(0)
            def scores(g, j):
                t, half = 8 * g + j, j // 4
                dve.wait_ge(s.s_done, t + 1)
                after(dve, s.p_done, t)
                if isinstance(t, int) and t == 0:
                    dve.wait_ge(s.q_first, 1)
                else:
                    dve.wait_ge(s.q_rsqrt, 2 * g + 1 + half)
                for h in range(R):
                    c = R * (j % 4) + h
                    ins = dve.scalar_tensor_tensor(out=sx[:, h, :], in0=pb[0][:, bass.ts(h, P)],
                                                   scalar=q_rstd[:, half, c:c + 1], in1=mask_sb[:],
                                                   op0=ALU.mult, op1=ALU.add)
                ins.then_inc(s.s_masked, 1)
                dve.wait_ge(s.s_masked, t + 1)
                dve.tensor_reduce(neg_max[:], sx[:], AX, ALU.max, negate=True).then_inc(s.s_max, 1)

            def normalise(t):
                dve.wait_ge(s.s_exp, t + 1)
                dve.reciprocal(rsum[:], esum[:]).then_inc(s.s_rsum, 1)
                dve.wait_ge(s.s_rsum, t + 1)
                after(dve, s.p_turned, t)
                dve.tensor_tensor(pr[:], sx[:], rsum[:].unsqueeze(2).to_broadcast([P, R, P]), ALU.mult).then_inc(s.p_done, 1)

            def p_rest(t):
                dve.wait_ge(s.p_hi_done, t + 1)
                rest(pt_lo[:], pb[1][:].rearrange("p (h t) -> p h t", h=R), pt_hi[:]).then_inc(s.p_lo_done, 1)

            def add_o(t, b):
                dve.wait_ge(s.o_done, t + 1)
                dve.tensor_tensor(x1[:, b, :], x1[:, b, :], pb[4][:], ALU.add).then_inc(s.o_added, 1)

            def attention_rest(t):
                dve.wait_ge(s.at_hi_done, t + 1)
                rest(at_lo[:], pb[3][:].rearrange("p (h t) -> p h t", h=R), at_hi[:]).then_inc(s.at_lo_done, 1)

            def step(g, j, first=False, last=False):
                t = 8 * g + j
                scores(g, j)
                if first and j == 0:
                    sq_rest(t + 5, (j + 1) % 2)
                if first and j == 1:
                    p_rest(t - 1)
                if j == 2 and not first:
                    wo_rest(g)
                normalise(t)
                if j == 3 or j == 7 and not last:
                    mean_q(2 * g + 1 + j // 4)
                if not (first and j < 2):
                    p_rest(t - 1)
                if (j < 3 or not last) and not (first and j == 0):
                    sq_rest(t + 5, (j + 1) % 2)
                if not (first and j < 2):
                    add_o(t - 2, (j - 2) % 8)
                if not (first and j < 1):
                    attention_rest(t - 1)

            for j in range(8):
                step(0, j, first=True)
            with dve.Fori(1, G - 1) as g:
                for j in range(8):
                    step(g, j)

            def x2_rest(b):
                save_lo(1, b, x2_hi, x2_lo, (2, 6)[b % 2])

            def stats_when_added(b):
                dve.wait_ge(s.o_added, LAST - B + b + 2)
                ln_stats(b)

            for j in range(3):
                step(G - 1, j, last=True)
            stats_when_added(0)
            mean_q(2 * G - 1)
            for j in range(3, 8):
                t = LAST - 7 + j
                scores(G - 1, j)
                p_rest(t - 1)
                add_o(t - 2, j - 2)
                b = j - 2
                dve.wait_ge(s.o_added, t - 1)
                dve.bn_stats(bn[:, b, :], x1[:, b, :]).then_inc(s.bn_done, 1)
                normalise(t)
                dve.wait_ge(s.bn_done, b)
                link(dve.bn_aggr(mv[:, b, :], bn[:, b, :]))
                dve.tensor_scalar(ve[:, b:b + 1], mv[:, b, 1:2], EPS, None, ALU.add).then_inc(s.ln_var, 1)
                attention_rest(t - 1)
                ln_apply(j, j - 3)
                if j >= 4:
                    x2_rest(j - 4)
            p_rest(LAST)
            add_o(LAST - 1, B - 2)
            stats_when_added(B - 2)
            attention_rest(LAST)
            ln_apply(8, 5)
            x2_rest(4)

            def hid_rest(unit, m):
                dve.wait_ge(s.hid_hi_done, KT * unit + m + 1)
                rest(hid_lo[:, m, :], hid[:, m % 2, :], hid_hi[:, m, :]).then_inc(s.hid_lo_done, 1)

            hid_rest(0, 0)
            add_o(LAST, B - 1)
            stats_when_added(B - 1)
            ln_apply(9, 6)
            x2_rest(5)
            hid_rest(0, 1)
            ln_apply(10, 7)
            x2_rest(6)
            hid_rest(0, 2)
            x2_rest(7)
            hid_rest(0, 3)

            dve.wait_ge(s.gate_dma, 16 * E)
            dve.wait_ge(s.ln_out, 2 * B)
            dve.wait_ge(s.row_sums, B)
            dve.wait_ge(s.o_done, LAST + 1)
            for i in range(E * B):
                e, b = i // B, i % B
                ins = dve.tensor_tensor_reduce((junk, junk_b)[i % 2][:], x1[:, b, :], gate_e[e], 1.0, 0.0,
                                               ALU.mult, ALU.add, gt[:, e, b:b + 1])
                if i % 2:
                    link(ins)
                if i in (15, 19, 23):
                    hid_rest(1, (i - 15) // 4)
            v = lambda n: gt[:, n, :]
            RATIO, VS, MX, SUM, T01 = 3, 12, 13, 14, 15
            dve.wait_ge(s.means, 1)
            link(dve.tensor_scalar(v(VS), pb[2][:, B:2 * B], 1e-8, None, ALU.add))
            link(dve.reciprocal(v(MX), v(VS)))
            link(dve.tensor_tensor(v(RATIO), pb[2][:, 0:B], v(MX), ALU.mult))
            for e in range(E):
                ins = dve.scalar_tensor_tensor(out=v(16 + e), in0=v(RATIO), scalar=gw_last[:, e:e + 1], in1=v(e),
                                               op0=ALU.mult, op1=ALU.add)
            link(ins)
            for e in range(E):
                ins = dve.tensor_scalar(v(19 + e), v(16 + e), gb_sb[:, e:e + 1], None, ALU.add)
            link(ins)
            by_batch = lambda a, z: gt[:, a:z, :].rearrange("p e b -> p b e")
            over_e = lambda n: v(n).unsqueeze(1).to_broadcast([P, E, B])
            link(dve.tensor_reduce(v(22), by_batch(19, 22), AX, ALU.max))
            dve.tensor_tensor(gt[:, 4:7, :], gt[:, 19:22, :], over_e(22), ALU.subtract).then_inc(s.g_sub, 1)
            hid_rest(1, 3)
            dve.wait_ge(s.g_exp, 1)
            link(dve.tensor_reduce(v(SUM), by_batch(8, 11), AX, ALU.add))
            link(dve.reciprocal(v(T01), v(SUM)))
            link(dve.tensor_tensor(gt[:, 23:26, :], gt[:, 8:11, :], over_e(T01), ALU.mult))
            a, b_, c = v(23), v(24), v(25)
            dve.tensor_tensor(v(26), a, b_, ALU.is_ge)
            dve.tensor_tensor(v(27), a, c, ALU.is_ge)
            link(dve.tensor_tensor(v(28), b_, c, ALU.is_ge))
            dve.tensor_tensor(v(32), v(26), v(27), ALU.add)
            dve.tensor_tensor(v(33), v(26), v(28), ALU.subtract)
            link(dve.tensor_tensor(v(31), v(27), v(28), ALU.add))
            dve.tensor_scalar(v(29), v(32), -1.0, 2.0, ALU.mult, ALU.add)
            link(dve.tensor_scalar(v(30), v(33), 1.0, None, ALU.add))
            dve.tensor_scalar(onehot[:, 0], gt[:, 29:32, :], 0.0, None, ALU.is_equal)
            dve.tensor_scalar(onehot[:, 1], gt[:, 29:32, :], 1.0, None, ALU.is_equal).then_inc(s.picked, 1)
            dve.wait_ge(s.picked, 1)
            for i in range(2):
                link(dve.tensor_tensor(gt[:, 34:37, :], onehot[:, i], gt[:, 23:26, :], ALU.mult))
                link(dve.tensor_reduce(v(37 + i), by_batch(34, 37), AX, ALU.add))
            link(dve.tensor_tensor(v(39), v(37), v(38), ALU.add))
            link(dve.tensor_scalar(v(34), v(39), 1e-8, None, ALU.add))
            link(dve.reciprocal(v(35), v(34)))
            link(dve.tensor_tensor(gt[:, 37:39, :], gt[:, 37:39, :], v(35).unsqueeze(1).to_broadcast([P, 2, B]), ALU.mult))
            dve.wait_ge(s.choice_out, 1)
            for i in range(2):
                link(dve.tensor_tensor(choice[:, i], pb[2][:, 16 + 24 * i:40 + 24 * i].rearrange("p (e b) -> p e b", e=E),
                                       v(37 + i).unsqueeze(1).to_broadcast([P, E, B]), ALU.mult))
            link(dve.tensor_tensor(coef[:], choice[:, 0], choice[:, 1], ALU.add))
            dve.wait_ge(s.b2_dma, 16 * E)

            def weigh(unit, t, src):
                b, e = 4 * (unit // E) + t, unit % E
                return dve.scalar_tensor_tensor(out=x1[:, b, :], in0=src, scalar=coef[:, e, b:b + 1],
                                                in1=x1[:, b, :], op0=ALU.mult, op1=ALU.add)

            def add_y(unit, t):
                if unit:
                    dve.wait_ge(s.y_done, 4 * unit + t + 1)
                else:
                    dve.wait_ge(s.y_saved, t + 1)
                weigh(unit, t, pb[Y_BANKS[t]][:] if unit else y_raw[:, t, :]).then_inc(s.y_added, 1)

            for unit in range(2 * E):
                if unit >= 2:
                    for m in range(KT):
                        hid_rest(unit, m)
                if unit == E:
                    for b in range(4):
                        ln_stats(b)
                    for b in range(4):
                        ln_apply(11 + b, b)
                for t in range(4):
                    ins = weigh(unit, t, b2_b[:, unit % E, :])
                link(ins)
                for t in range(4):
                    add_y(unit, t)
                    if unit == 2 * E - 1:
                        dve.wait_ge(s.y_added, 4 * unit + t + 1)
                        ln_stats(4 + t)
                        if t:
                            ln_apply(14 + t, 3 + t)
                dve.wait_ge(s.y_added, 4 * unit + 4)
            ln_apply(18, 7)

        @block.tensor
        def _(pe):
            def three(out_ap, pairs):
                n = 3 * len(pairs)
                i = 0
                for w_hi, w_lo, m_hi, m_lo in pairs:
                    for w, m in ((w_hi, m_hi), (w_hi, m_lo), (w_lo, m_hi)):
                        ins = pe.matmul(out_ap, w, m, start=(i == 0), stop=(i == n - 1))
                        i += 1
                return ins

            def project(hi, lo, u, half, bank_):
                cols_ = bass.ts(half, 512)
                return three(pb[bank_][:], [(ctx_hi[:, u, bass.ts(k, P)], ctx_lo[:, u, bass.ts(k, P)],
                                             hi[:, k, cols_], lo[:, k, cols_]) for k in range(KT)])

            def turn_keys(i, half):
                if half == 0:
                    pe.wait_ge(s.k_normed, i + 1)
                after(pe, s.k_saved, 2 * i + half)
                for c in range(4):
                    ins = pe.transpose(pb[5][:, bass.ts(c, P)], k_raw[:, 4 * half + c, :], ident[:])
                ins.then_inc(s.k_turned, 1)

            def values(i, u, first=False):
                after(pe, s.v_saved, 2 * i)
                for half in range(2):
                    if first:
                        pe.wait_ge(s.kv_lo_done, 12 + 4 * half)
                    project(wv_hi, wv_lo, u, half, 6 + half).then_inc(s.v_done, 1)

            def chunk(turn, u, first=False):
                i = 2 * turn + u
                pe.wait_ge(s.cols_dma[u], 16 * turn + 16)
                after(pe, s.a_extracted, i)
                for c in range(CG):
                    w = cols[:, u, bass.ts(c, P)]
                    ins = pe.matmul(pb[0][:, bass.ts(c, P)], w, w, start=True, stop=True)
                ins.then_inc(s.a_scores, 1)

                def keys(half):
                    if half == 0:
                        pe.wait_ge(s.ctx_lo_done, i + 1)
                        after(pe, s.k_raw_done, 3 * i)
                    if first:
                        pe.wait_ge(s.kv_lo_done, 4 + 4 * half)
                    ins = project(wk_hi, wk_lo, u, half, 3 + half)
                    if half == 1:
                        ins.then_inc(s.projected, 1)

                def turn_probs():
                    pe.wait_ge(s.a_probs, i + 1)
                    for c in range(CG):
                        ins = pe.transpose(pb[1][:, bass.ts(c, P)], block_p[:, c, :], ident[:])
                    ins.then_inc(s.a_turned, 1)

                def messages():
                    pe.wait_ge(s.a_probs_t, i + 1)
                    pe.wait_ge(s.rows_dma[u], 16 * turn + 16)
                    after(pe, s.a_added, i)
                    for c in range(CG):
                        ins = pe.matmul(pb[2][:, bass.ts(c, P)], rows[:, u, bass.ts(c, P)], block_pt[:, c, :],
                                        start=True, stop=True)
                    ins.then_inc(s.a_msg, 1)

                if first:
                    keys(0)
                    turn_probs()
                    keys(1)
                    messages()
                else:
                    values(i - 1, (u + 1) % 2, first=isinstance(i, int))
                    turn_probs()
                    keys(0)
                    messages()
                    turn_keys(i - 1, 0)
                    keys(1)
                    turn_keys(i - 1, 1)

            pe.wait_ge(s.consts, 1)
            chunk(0, 0, first=True)
            chunk(0, 1)
            with pe.Fori(1, CH // 2) as turn:
                chunk(turn, 0)
                chunk(turn, 1)

            def turn_x(n, b, banks):
                pe.wait_ge(s.ln_out, B * n + b + 1)
                if b >= len(banks) or n:
                    pe.wait_ge(s.x_lo_done, B * n + b + 1 - len(banks))
                for k in range(KT):
                    ins = pe.transpose(pb[banks[b % len(banks)]][:, bass.ts(k, P)], x1[:, b, bass.ts(k, P)], ident[:])
                ins.then_inc(s.x_turned, 1)

            pe.wait_ge(s.v_saved, 2 * B - 2)
            project(wv_hi, wv_lo, 1, 0, 6).then_inc(s.v_done, 1)
            for b in range(4):
                if b == 2:
                    pe.wait_ge(s.k_raw_done, 3 * B)
                turn_x(0, b, X_BANKS)
            project(wv_hi, wv_lo, 1, 1, 7).then_inc(s.v_done, 1)

            def query_piece(g, n, half, h, parity):
                pe.wait_ge(s.wq_lo_done, 4 * g + h + 1)
                after(pe, s.q_sq_lo_done, n - 1)
                cols_ = bass.ts(half, HALF_T)
                three(pb[(2, 6)[parity]][:], [(wq_hi[:, h, k, :], wq_lo[:, h, k, :], x_hi[:, k, cols_], x_lo[:, k, cols_])
                                              for k in range(KT)]).then_inc(s.q_done, 1)

            def query_sums(n, hh, h):
                pe.wait_ge(s.q_sq_lo_done, n + 1)
                if h == 0:
                    after(pe, s.q_row_saved, hh)
                pe.matmul(pb[5][:], head_row[:, h, :], q_sq_hi[:], start=(h == 0), stop=False)
                pe.matmul(pb[5][:], head_row[:, h, :], q_sq_lo[:], start=False, stop=(h == R - 1)).then_inc(s.q_summed, 1)

            def turn_sums(hh):
                pe.wait_ge(s.q_row_saved, hh + 1)
                after(pe, s.q_mean, hh)
                for c in range(4):
                    ins = pe.transpose(pb[7][:, bass.ts(c, P)], q_row[:, bass.ts(c, P)], ident[:])
                ins.then_inc(s.q_sums_turned, 1)

            pe.wait_ge(s.x_lo_done, 4)
            pe.wait_ge(s.v_saved, 2 * B)
            query_piece(0, 0, 0, 0, 0)
            turn_x(0, 4, X_BANKS)
            turn_x(0, 5, X_BANKS)
            turn_keys(B - 1, 0)
            query_piece(0, 1, 0, 1, 1)
            turn_keys(B - 1, 1)
            turn_x(0, 6, X_BANKS)
            turn_x(0, 7, X_BANKS)
            pe.wait_ge(s.k_saved, 2 * B)
            pe.wait_ge(s.consts, 3)
            query_sums(0, 0, 0)
            for n in range(2, 5):
                if n == 4:
                    pe.wait_ge(s.x_lo_done, B)
                query_piece(0, n, n // 4, n % 4, n % 2)
                query_sums(n - 1, 0, n - 1)
            turn_sums(0)

            def scores(g, j):
                t, half = 8 * g + j, j // 4
                pe.wait_ge(s.q_saved, 8 * g + 4 + 4 * half)
                after(pe, s.s_masked, t)
                for h in range(R):
                    ins = pe.matmul(pb[0][:, bass.ts(h, P)], q_t[:, half, h, bass.ts(j % 4, P)],
                                    k_t[:, bass.ds(g, 1), bass.ts(j, P)].rearrange("p a t -> p (a t)"),
                                    start=True, stop=True)
                ins.then_inc(s.s_done, 1)

            def turn_p(t):
                pe.wait_ge(s.p_done, t + 1)
                after(pe, s.p_lo_done, t)
                for h in range(R):
                    ins = pe.transpose(pb[1][:, bass.ts(h, P)], pr[:, h, :], ident[:])
                ins.then_inc(s.p_turned, 1)

            def attend(t, g, b):
                pe.wait_ge(s.p_lo_done, t + 1)
                pe.wait_ge(s.v_lo_done, 2 * g + 1 + b // 4)
                after(pe, s.at_lo_done, t)
                flat = lambda a: a[:].rearrange("p h t -> p (h t)")
                three(pb[3][:], [(v_hi[:, b, :], v_lo[:, b, :], flat(pt_hi), flat(pt_lo))]).then_inc(s.pv_done, 1)

            def project_out(t, g):
                pe.wait_ge(s.at_lo_done, t + 1)
                pe.wait_ge(s.wo_lo_done, 2 * g + 2)
                pe.wait_ge(s.wo2_lo_done, 2 * g + 2)
                after(pe, s.o_added, t)
                three(pb[4][:], [(at_hi[:, h, :], at_lo[:, h, :], wo_hi[:, h, :], wo_lo[:, h, :])
                                 for h in range(R)]).then_inc(s.o_done, 1)

            def step(g, j, first=False, last=False):
                t = 8 * g + j
                n = t + 5
                piece = j < 3 or not last
                scores(g, j)
                if first and j == 2:
                    attend(0, 0, 0)
                if first and j in (1, 2):
                    query_piece(g, n, *PIECE[j], (j + 1) % 2)
                query_sums(n - 1, 2 * g + 1 + j // 4, j % 4)
                if piece and not (first and j in (1, 2)):
                    query_piece(g if j < 3 else g + 1, n, *PIECE[j], (j + 1) % 2)
                if j == 3 or j == 7 and not last:
                    turn_sums(2 * g + 1 + j // 4)
                if not (first and j < 1):
                    turn_p(t - 1)
                if not (first and j < 2):
                    project_out(t - 2, g if j > 1 else g - 1)
                if not (first and j < 2):
                    attend(t - 1, g if j > 0 else g - 1, (j - 1) % 8)

            for j in range(8):
                step(0, j, first=True)
            with pe.Fori(1, G - 1) as g:
                for j in range(8):
                    step(g, j)
            for j in range(3):
                step(G - 1, j, last=True)
            scores(G - 1, 3)
            query_sums(8 * G - 1, 2 * G - 1, R - 1)
            turn_sums(2 * G - 1)
            for j in range(3, 8):
                t = LAST - 7 + j
                turn_p(t - 1)
                project_out(t - 2, G - 1)
                if j < 7:
                    scores(G - 1, j + 1)
                if j >= 4:
                    turn_x(1, j - 4, (2, 6))
                attend(t - 1, G - 1, j - 1)

            def before_activation(unit, m):
                half, e = unit // E, unit % E
                n = KT * unit + m
                pe.wait_ge(s.ff_lo_done, ff_index[0, e, KT - 1] + 1)
                pe.wait_ge(s.x_lo_done, B + 4 + 4 * half)
                after(pe, s.act_done, n - 1)
                cols_ = bass.ts(half, HALF_T)
                three(pb[m % 2][:], [(w1_hi[e][:, k, bass.ts(m, P)], w1_lo[e][:, k, bass.ts(m, P)],
                                      x2_hi[:, k, cols_], x2_lo[:, k, cols_]) for k in range(KT)]).then_inc(s.pre_done, 1)

            def output(e, m, t, finish):
                for i, (w, r) in enumerate(((hid_hi, w2_hi), (hid_hi, w2_lo), (hid_lo, w2_hi))):
                    ins = pe.matmul(pb[Y_BANKS[t]][:], w[:, m, bass.ts(t, P)], r[e][:, m, :],
                                    start=(m == 0 and i == 0), stop=(finish and i == 2))
                if finish:
                    ins.then_inc(s.y_done, 1)

            turn_p(LAST)
            project_out(LAST - 1, G - 1)
            turn_x(1, 4, (2, 6))
            attend(LAST, G - 1, B - 1)
            before_activation(0, 0)
            turn_x(1, 5, (2, 6))
            project_out(LAST, G - 1)
            before_activation(0, 1)
            turn_x(1, 6, (2, 6))
            before_activation(0, 2)
            turn_x(1, 7, (2, 6))
            before_activation(0, 3)
            pe.wait_ge(s.o_added, LAST + 1)

            for unit in range(2 * E):
                e = unit % E
                if unit:
                    for m in range(KT):
                        before_activation(unit, m)
                pe.wait_ge(s.ff_lo_done, ff_index[1, e, KT - 1] + 1)
                if unit == 1:
                    pe.wait_ge(s.y_saved, 4)
                elif unit:
                    pe.wait_ge(s.y_added, 4 * unit)
                if unit < 2 * E - 1:
                    for m in range(KT):
                        if unit == 1 and m == KT - 1:
                            pe.wait_ge(s.picked, 1)
                            pe.matmul(pb[2][:, 16:64], row0[:], onehot[:].rearrange("p i e b -> p (i e b)"),
                                      start=True, stop=True).then_inc(s.choice_out, 1)
                        pe.wait_ge(s.hid_lo_done, KT * unit + m + 1)
                        for t in range(4):
                            output(e, m, t, m == KT - 1)
                        if unit == 0 and m == 0:
                            pe.wait_ge(s.row_sums, B)
                            pe.wait_ge(s.x_lo_done, 2 * B)
                            pe.matmul(pb[2][:, 0:B], text_mean[:], row_abs[:], start=True, stop=True)
                            pe.matmul(pb[2][:, B:2 * B], vis_mean[:], row_abs[:], start=True,
                                      stop=True).then_inc(s.means, 1)
                else:
                    for t in range(4):
                        for m in range(KT):
                            if t == 0:
                                pe.wait_ge(s.hid_lo_done, KT * unit + m + 1)
                            output(e, m, t, m == KT - 1)


def kernel(**inputs):
    import numpy as np
    import concourse.bacc as bacc
    from concourse.bass_utils import run_bass_kernel_spmd as run

    a = {n: np.asarray(v) for n, v in inputs.items()}
    x = a["x"]
    wk, wv = a["L0_xattn_k_proj_w"], a["L0_xattn_v_proj_w"]
    w2t = lambda w: w.reshape(2, 512, KT, P).transpose(3, 2, 0, 1)
    arrays = {
        "x_nat": x,
        "x_cols": x.transpose(1, 2, 0).reshape(P, CH, CL * B).transpose(1, 0, 2),
        "x_rows": x.transpose(2, 0, 1).reshape(CH, CG, P, P).transpose(0, 2, 1, 3).reshape(CH, P, CG * P),
        "ctx_t": a["ctx_4096"].reshape(B, P, KT, P).transpose(0, 3, 2, 1).reshape(B, P, KT * P),
        "mask": a["mask_1x1xSxS2_ff0"].reshape(P, P),
        "wq_t": a["L0_xattn_q_proj_w"].reshape(G * R, P, KT, P).transpose(0, 3, 2, 1).reshape(G * R, P, KT * P),
        "wkv_t": np.stack([w2t(w)[:, k, half] for w in (wk, wv) for half in range(2) for k in range(KT)]),
        "wo_t": a["L0_xattn_o_proj_w"].T.reshape(G, R, P, D).transpose(0, 2, 1, 3),
        "qn_w": a["L0_xattn_q_norm_w"], "kn_w": a["L0_xattn_k_norm_w"],
        "gate_wt": a["L0_ffn_gate_w"][:D].T, "gate_last": a["L0_ffn_gate_w"][D], "gate_b": a["L0_ffn_gate_b"],
        "w1": a["L0_ffn_w1"], "b1_t": a["L0_ffn_b1"].reshape(E, KT, P).transpose(2, 0, 1),
        "w2": a["L0_ffn_w2"], "b2": a["L0_ffn_b2"],
    }
    arrays = {n: np.ascontiguousarray(v) for n, v in arrays.items()}
    nc = bacc.Bacc("TRN2", target_bir_lowering=False, num_devices=1)
    aps = [nc.dram_tensor(n, v.shape, F32, kind="ExternalInput").ap() for n, v in arrays.items()]
    out = nc.dram_tensor("out", (B, P, D), F32, kind="ExternalOutput").ap()
    build(nc, *aps, out)
    r = run(nc, [arrays], core_ids=[0])
    return r.results[0]["out"]
```
